# Optimizing a Trainium2 kernel written in Bass

```python
import numpy as np
import jax
import jax.numpy as jnp

def _softmax(x, axis=-1):
    return jax.nn.softmax(x, axis=axis)

def _gelu(x):
    return jax.nn.gelu(x, approximate=True)

def _silu(x):
    return jax.nn.silu(x)

def _sigmoid(x):
    return jax.nn.sigmoid(x)

def _layernorm(x, axis=-1, eps=1e-05):
    m = jnp.mean(x, axis=axis, keepdims=True)
    v = jnp.var(x, axis=axis, keepdims=True)
    return (x - m) / jnp.sqrt(v + eps)

def _scatter_add(tgt, idx, src, axis=0):
    return tgt.at[idx].add(src)

def _segment_sum(src, seg, n):
    return jax.ops.segment_sum(src, seg, n)
kernel_name = 'mk_xattn_seq_d2_seqx_r4_ddf4c1'

def setup_inputs(seed: int=0):
    np.random.seed(seed)
    _w = jnp.asarray

    def _rec_inputs():
        import jax
        import jax.numpy as jnp
        _rk = jax.random.key(seed)
        x = 7.22e-05 + 1 * jax.random.normal(jax.random.fold_in(_rk, 1), (4, 512, 256), jnp.float32)
        _lenS = 512 - jax.random.randint(jax.random.fold_in(_rk, 7), (4,), 0, max(1, 512 // 4) + 1, jnp.int32)
        _lenS2 = 1601 - jax.random.randint(jax.random.fold_in(_rk, 8), (4,), 0, max(1, 1601 // 4) + 1, jnp.int32)
        _ctx_768P = jax.random.normal(jax.random.fold_in(_rk, 11), (4, 16, 192), jnp.float32)
        _ctx_768c = jax.random.dirichlet(jax.random.fold_in(_rk, 511), 0.3 * jnp.ones((16,), jnp.float32), (4, 1601))
        _ctx_768t = jnp.einsum('bsk,bkd->bsd', _ctx_768c, _ctx_768P)
        _ctx_768t = _ctx_768t * jax.lax.rsqrt(jnp.mean(jnp.square(_ctx_768t)) + 1e-12) * 0.953939
        ctx_768 = 0.000651243 + 0.998673 * (_ctx_768t + 0.3 * jax.random.normal(jax.random.fold_in(_rk, 611), (4, 1601, 192), jnp.float32))
        return (x, ctx_768)
    x, ctx_768 = _rec_inputs()

    def _L0_xattn_setup():
        import jax, jax.numpy as jnp
        import numpy as np
        HEADS = 16
        D_HEAD = 64
        EPS = 1e-05

        def _ln(x, g, b):
            m = jnp.mean(x, axis=-1, keepdims=True)
            v = jnp.var(x, axis=-1, keepdims=True)
            return (x - m) * jax.lax.rsqrt(v + EPS) * g + b

        def _attn(xq, xc, Wq, Wk, Wv, Wo, bo):
            B, N, _ = xq.shape
            S = xc.shape[1]
            q = (xq @ Wq).reshape(B, N, HEADS, D_HEAD)
            k = (xc @ Wk).reshape(B, S, HEADS, D_HEAD)
            v = (xc @ Wv).reshape(B, S, HEADS, D_HEAD)
            scale = D_HEAD ** (-0.5)
            scores = jnp.einsum('bnhd,bshd->bhns', q, k) * scale
            attn = jax.nn.softmax(scores, axis=-1)
            out = jnp.einsum('bhns,bshd->bnhd', attn, v).reshape(B, N, HEADS * D_HEAD)
            return out @ Wo + bo

        def _geglu_ff(x, Wp, bp, Wf, bf):
            h = x @ Wp + bp
            a, gate = jnp.split(h, 2, axis=-1)
            return a * jax.nn.gelu(gate, approximate=False) @ Wf + bf
        key = jax.random.key(seed)
        ks = jax.random.split(key, 16)
        dim, ctx, inner, ffin = (256, 192, HEADS * D_HEAD, 4 * 256)

        def w(k, i, o):
            return jax.random.normal(k, (i, o), jnp.float32) * i ** (-0.5)
        inp = {'x': jax.random.normal(ks[0], (4, 512, dim), jnp.float32), 'context': jax.random.normal(ks[1], (4, 77, ctx), jnp.float32), 'Wq1': w(ks[2], dim, inner), 'Wk1': w(ks[3], dim, inner), 'Wv1': w(ks[4], dim, inner), 'Wo1': w(ks[5], inner, dim), 'bo1': jnp.zeros((dim,), jnp.float32), 'Wq2': w(ks[6], dim, inner), 'Wk2': w(ks[7], ctx, inner), 'Wv2': w(ks[8], ctx, inner), 'Wo2': w(ks[9], inner, dim), 'bo2': jnp.zeros((dim,), jnp.float32), 'Wp': w(ks[10], dim, 2 * ffin), 'bp': jnp.zeros((2 * ffin,), jnp.float32), 'Wf': w(ks[11], ffin, dim), 'bf': jnp.zeros((dim,), jnp.float32), 'g1': jnp.ones((dim,), jnp.float32), 'b1': jnp.zeros((dim,), jnp.float32), 'g2': jnp.ones((dim,), jnp.float32), 'b2': jnp.zeros((dim,), jnp.float32), 'g3': jnp.ones((dim,), jnp.float32), 'b3': jnp.zeros((dim,), jnp.float32)}
        return inp
    _L0_xattn_all = _L0_xattn_setup()
    _L0_xattn_in = {k: v for k, v in _L0_xattn_all.items() if k in ('Wq1', 'Wk1', 'Wv1', 'Wo1', 'bo1', 'Wq2', 'Wk2', 'Wv2', 'Wo2', 'bo2', 'Wp', 'bp', 'Wf', 'bf', 'g1', 'b1', 'g2', 'b2', 'g3', 'b3')}
    del _L0_xattn_all

    def _L1_xattn_setup():
        import jax, jax.numpy as jnp
        import numpy as np
        EPS = 1e-05

        def _ln(x, g, b):
            m = jnp.mean(x, axis=-1, keepdims=True)
            v = jnp.var(x, axis=-1, keepdims=True)
            return (x - m) * jax.lax.rsqrt(v + EPS) * g + b

        def _attn(x, ctx, wq, wk, wv, wo, bo, num_heads):
            B, T, _ = x.shape
            S = ctx.shape[1]
            E = wq.shape[1]
            hd = E // num_heads
            q = (x @ wq).reshape(B, T, num_heads, hd)
            k = (ctx @ wk).reshape(B, S, num_heads, hd)
            v = (ctx @ wv).reshape(B, S, num_heads, hd)
            scores = jnp.einsum('bthd,bshd->bhts', q, k) / np.sqrt(hd).astype(x.dtype)
            p = jax.nn.softmax(scores, axis=-1)
            o = jnp.einsum('bhts,bshd->bthd', p, v).reshape(B, T, E)
            return o @ wo + bo

        def _ffn(x, w1, b1, w2, b2):
            h = jax.nn.gelu(x @ w1 + b1, approximate=False)
            return h @ w2 + b2
        key = jax.random.key(seed)
        H, CD, FF = (256, 192, 1024)
        ks = jax.random.split(key, 20)
        s = 0.02
        inp = {'x': jax.random.normal(ks[0], (4, 256, H), jnp.float32), 'context': jax.random.normal(ks[1], (4, 77, CD), jnp.float32), 'sq_w': jax.random.normal(ks[2], (H, H), jnp.float32) * s, 'sk_w': jax.random.normal(ks[3], (H, H), jnp.float32) * s, 'sv_w': jax.random.normal(ks[4], (H, H), jnp.float32) * s, 'so_w': jax.random.normal(ks[5], (H, H), jnp.float32) * s, 'so_b': jnp.zeros((H,), jnp.float32), 'cq_w': jax.random.normal(ks[6], (H, H), jnp.float32) * s, 'ck_w': jax.random.normal(ks[7], (CD, H), jnp.float32) * s, 'cv_w': jax.random.normal(ks[8], (CD, H), jnp.float32) * s, 'co_w': jax.random.normal(ks[9], (H, H), jnp.float32) * s, 'co_b': jnp.zeros((H,), jnp.float32), 'n1_g': jnp.ones((H,), jnp.float32), 'n1_b': jnp.zeros((H,), jnp.float32), 'n2_g': jnp.ones((H,), jnp.float32), 'n2_b': jnp.zeros((H,), jnp.float32), 'n3_g': jnp.ones((H,), jnp.float32), 'n3_b': jnp.zeros((H,), jnp.float32), 'n4_g': jnp.ones((H,), jnp.float32), 'n4_b': jnp.zeros((H,), jnp.float32), 'f1_w1': jax.random.normal(ks[10], (H, FF), jnp.float32) * s, 'f1_b1': jnp.zeros((FF,), jnp.float32), 'f1_w2': jax.random.normal(ks[11], (FF, H), jnp.float32) * s, 'f1_b2': jnp.zeros((H,), jnp.float32), 'f2_w1': jax.random.normal(ks[12], (H, FF), jnp.float32) * s, 'f2_b1': jnp.zeros((FF,), jnp.float32), 'f2_w2': jax.random.normal(ks[13], (FF, H), jnp.float32) * s, 'f2_b2': jnp.zeros((H,), jnp.float32)}
        return inp
    _L1_xattn_all = _L1_xattn_setup()
    _L1_xattn_in = {k: v for k, v in _L1_xattn_all.items() if k in ('sq_w', 'sk_w', 'sv_w', 'so_w', 'so_b', 'cq_w', 'ck_w', 'cv_w', 'co_w', 'co_b', 'n1_g', 'n1_b', 'n2_g', 'n2_b', 'n3_g', 'n3_b', 'n4_g', 'n4_b', 'f1_w1', 'f1_b1', 'f1_w2', 'f1_b2', 'f2_w1', 'f2_b1', 'f2_w2', 'f2_b2')}
    del _L1_xattn_all
    return {'x': x, 'ctx_768': ctx_768, 'L0_xattn_Wq1': _L0_xattn_in['Wq1'], 'L0_xattn_Wk1': _L0_xattn_in['Wk1'], 'L0_xattn_Wv1': _L0_xattn_in['Wv1'], 'L0_xattn_Wo1': _L0_xattn_in['Wo1'], 'L0_xattn_bo1': _L0_xattn_in['bo1'], 'L0_xattn_Wq2': _L0_xattn_in['Wq2'], 'L0_xattn_Wk2': _L0_xattn_in['Wk2'], 'L0_xattn_Wv2': _L0_xattn_in['Wv2'], 'L0_xattn_Wo2': _L0_xattn_in['Wo2'], 'L0_xattn_bo2': _L0_xattn_in['bo2'], 'L0_xattn_Wp': _L0_xattn_in['Wp'], 'L0_xattn_bp': _L0_xattn_in['bp'], 'L0_xattn_Wf': _L0_xattn_in['Wf'], 'L0_xattn_bf': _L0_xattn_in['bf'], 'L0_xattn_g1': _L0_xattn_in['g1'], 'L0_xattn_b1': _L0_xattn_in['b1'], 'L0_xattn_g2': _L0_xattn_in['g2'], 'L0_xattn_b2': _L0_xattn_in['b2'], 'L0_xattn_g3': _L0_xattn_in['g3'], 'L0_xattn_b3': _L0_xattn_in['b3'], 'L1_xattn_sq_w': _L1_xattn_in['sq_w'], 'L1_xattn_sk_w': _L1_xattn_in['sk_w'], 'L1_xattn_sv_w': _L1_xattn_in['sv_w'], 'L1_xattn_so_w': _L1_xattn_in['so_w'], 'L1_xattn_so_b': _L1_xattn_in['so_b'], 'L1_xattn_cq_w': _L1_xattn_in['cq_w'], 'L1_xattn_ck_w': _L1_xattn_in['ck_w'], 'L1_xattn_cv_w': _L1_xattn_in['cv_w'], 'L1_xattn_co_w': _L1_xattn_in['co_w'], 'L1_xattn_co_b': _L1_xattn_in['co_b'], 'L1_xattn_n1_g': _L1_xattn_in['n1_g'], 'L1_xattn_n1_b': _L1_xattn_in['n1_b'], 'L1_xattn_n2_g': _L1_xattn_in['n2_g'], 'L1_xattn_n2_b': _L1_xattn_in['n2_b'], 'L1_xattn_n3_g': _L1_xattn_in['n3_g'], 'L1_xattn_n3_b': _L1_xattn_in['n3_b'], 'L1_xattn_n4_g': _L1_xattn_in['n4_g'], 'L1_xattn_n4_b': _L1_xattn_in['n4_b'], 'L1_xattn_f1_w1': _L1_xattn_in['f1_w1'], 'L1_xattn_f1_b1': _L1_xattn_in['f1_b1'], 'L1_xattn_f1_w2': _L1_xattn_in['f1_w2'], 'L1_xattn_f1_b2': _L1_xattn_in['f1_b2'], 'L1_xattn_f2_w1': _L1_xattn_in['f2_w1'], 'L1_xattn_f2_b1': _L1_xattn_in['f2_b1'], 'L1_xattn_f2_w2': _L1_xattn_in['f2_w2'], 'L1_xattn_f2_b2': _L1_xattn_in['f2_b2']}

def reference(x, ctx_768, L0_xattn_Wq1, L0_xattn_Wk1, L0_xattn_Wv1, L0_xattn_Wo1, L0_xattn_bo1, L0_xattn_Wq2, L0_xattn_Wk2, L0_xattn_Wv2, L0_xattn_Wo2, L0_xattn_bo2, L0_xattn_Wp, L0_xattn_bp, L0_xattn_Wf, L0_xattn_bf, L0_xattn_g1, L0_xattn_b1, L0_xattn_g2, L0_xattn_b2, L0_xattn_g3, L0_xattn_b3, L1_xattn_sq_w, L1_xattn_sk_w, L1_xattn_sv_w, L1_xattn_so_w, L1_xattn_so_b, L1_xattn_cq_w, L1_xattn_ck_w, L1_xattn_cv_w, L1_xattn_co_w, L1_xattn_co_b, L1_xattn_n1_g, L1_xattn_n1_b, L1_xattn_n2_g, L1_xattn_n2_b, L1_xattn_n3_g, L1_xattn_n3_b, L1_xattn_n4_g, L1_xattn_n4_b, L1_xattn_f1_w1, L1_xattn_f1_b1, L1_xattn_f1_w2, L1_xattn_f1_b2, L1_xattn_f2_w1, L1_xattn_f2_b1, L1_xattn_f2_w2, L1_xattn_f2_b2):
    import jax
    import jax.numpy as jnp

    def _L0_xattn_ref(x, context, Wq1, Wk1, Wv1, Wo1, bo1, Wq2, Wk2, Wv2, Wo2, bo2, Wp, bp, Wf, bf, g1, b1, g2, b2, g3, b3):
        import jax, jax.numpy as jnp
        import numpy as np
        HEADS = 16
        D_HEAD = 64
        EPS = 1e-05

        def _ln(x, g, b):
            m = jnp.mean(x, axis=-1, keepdims=True)
            v = jnp.var(x, axis=-1, keepdims=True)
            return (x - m) * jax.lax.rsqrt(v + EPS) * g + b

        def _attn(xq, xc, Wq, Wk, Wv, Wo, bo):
            B, N, _ = xq.shape
            S = xc.shape[1]
            q = (xq @ Wq).reshape(B, N, HEADS, D_HEAD)
            k = (xc @ Wk).reshape(B, S, HEADS, D_HEAD)
            v = (xc @ Wv).reshape(B, S, HEADS, D_HEAD)
            scale = D_HEAD ** (-0.5)
            scores = jnp.einsum('bnhd,bshd->bhns', q, k) * scale
            attn = jax.nn.softmax(scores, axis=-1)
            out = jnp.einsum('bhns,bshd->bnhd', attn, v).reshape(B, N, HEADS * D_HEAD)
            return out @ Wo + bo

        def _geglu_ff(x, Wp, bp, Wf, bf):
            h = x @ Wp + bp
            a, gate = jnp.split(h, 2, axis=-1)
            return a * jax.nn.gelu(gate, approximate=False) @ Wf + bf
        x = _attn(_ln(x, g1, b1), _ln(x, g1, b1), Wq1, Wk1, Wv1, Wo1, bo1) + x
        x = _attn(_ln(x, g2, b2), context, Wq2, Wk2, Wv2, Wo2, bo2) + x
        x = _geglu_ff(_ln(x, g3, b3), Wp, bp, Wf, bf) + x
        return x

    def _L1_xattn_ref(x, context, sq_w, sk_w, sv_w, so_w, so_b, cq_w, ck_w, cv_w, co_w, co_b, n1_g, n1_b, n2_g, n2_b, n3_g, n3_b, n4_g, n4_b, f1_w1, f1_b1, f1_w2, f1_b2, f2_w1, f2_b1, f2_w2, f2_b2):
        import jax, jax.numpy as jnp
        import numpy as np
        EPS = 1e-05

        def _ln(x, g, b):
            m = jnp.mean(x, axis=-1, keepdims=True)
            v = jnp.var(x, axis=-1, keepdims=True)
            return (x - m) * jax.lax.rsqrt(v + EPS) * g + b

        def _attn(x, ctx, wq, wk, wv, wo, bo, num_heads):
            B, T, _ = x.shape
            S = ctx.shape[1]
            E = wq.shape[1]
            hd = E // num_heads
            q = (x @ wq).reshape(B, T, num_heads, hd)
            k = (ctx @ wk).reshape(B, S, num_heads, hd)
            v = (ctx @ wv).reshape(B, S, num_heads, hd)
            scores = jnp.einsum('bthd,bshd->bhts', q, k) / np.sqrt(hd).astype(x.dtype)
            p = jax.nn.softmax(scores, axis=-1)
            o = jnp.einsum('bhts,bshd->bthd', p, v).reshape(B, T, E)
            return o @ wo + bo

        def _ffn(x, w1, b1, w2, b2):
            h = jax.nn.gelu(x @ w1 + b1, approximate=False)
            return h @ w2 + b2
        NUM_HEADS = 16
        x = _attn(_ln(x, n1_g, n1_b), _ln(x, n1_g, n1_b), sq_w, sk_w, sv_w, so_w, so_b, NUM_HEADS) + x
        x = _ffn(_ln(x, n2_g, n2_b), f1_w1, f1_b1, f1_w2, f1_b2) + x
        x = _attn(_ln(x, n3_g, n3_b), context, cq_w, ck_w, cv_w, co_w, co_b, NUM_HEADS) + x
        x = _ffn(_ln(x, n4_g, n4_b), f2_w1, f2_b1, f2_w2, f2_b2) + x
        return x
    x = _L0_xattn_ref(x, ctx_768, L0_xattn_Wq1, L0_xattn_Wk1, L0_xattn_Wv1, L0_xattn_Wo1, L0_xattn_bo1, L0_xattn_Wq2, L0_xattn_Wk2, L0_xattn_Wv2, L0_xattn_Wo2, L0_xattn_bo2, L0_xattn_Wp, L0_xattn_bp, L0_xattn_Wf, L0_xattn_bf, L0_xattn_g1, L0_xattn_b1, L0_xattn_g2, L0_xattn_b2, L0_xattn_g3, L0_xattn_b3)
    x = _L1_xattn_ref(x, ctx_768, L1_xattn_sq_w, L1_xattn_sk_w, L1_xattn_sv_w, L1_xattn_so_w, L1_xattn_so_b, L1_xattn_cq_w, L1_xattn_ck_w, L1_xattn_cv_w, L1_xattn_co_w, L1_xattn_co_b, L1_xattn_n1_g, L1_xattn_n1_b, L1_xattn_n2_g, L1_xattn_n2_b, L1_xattn_n3_g, L1_xattn_n3_b, L1_xattn_n4_g, L1_xattn_n4_b, L1_xattn_f1_w1, L1_xattn_f1_b1, L1_xattn_f1_w2, L1_xattn_f1_b2, L1_xattn_f2_w1, L1_xattn_f2_b1, L1_xattn_f2_w2, L1_xattn_f2_b2)
    return x

_drawn_inputs = setup_inputs


def setup_inputs(seed=0):
    import zlib

    import numpy as np

    out = dict(_drawn_inputs(seed))
    spreads = {'L0_xattn_bo1': (0.0, 0.1),
     'L0_xattn_bo2': (0.0, 0.1),
     'L0_xattn_bp': (0.0, 0.1),
     'L0_xattn_bf': (0.0, 0.1),
     'L0_xattn_g1': (1.0, 0.2),
     'L0_xattn_b1': (0.0, 0.1),
     'L0_xattn_g2': (1.0, 0.2),
     'L0_xattn_b2': (0.0, 0.408),
     'L0_xattn_g3': (1.0, 0.2),
     'L0_xattn_b3': (0.0, 0.1),
     'L1_xattn_so_b': (0.0, 0.1),
     'L1_xattn_co_b': (0.0, 0.1),
     'L1_xattn_n1_g': (1.0, 0.6),
     'L1_xattn_n1_b': (0.0, 0.8),
     'L1_xattn_n2_g': (1.0, 0.6),
     'L1_xattn_n2_b': (0.0, 0.8),
     'L1_xattn_n3_g': (1.0, 0.6),
     'L1_xattn_n3_b': (0.0, 0.8),
     'L1_xattn_n4_g': (1.0, 0.6),
     'L1_xattn_n4_b': (0.0, 0.8),
     'L1_xattn_f1_b1': (0.0, 0.322),
     'L1_xattn_f1_b2': (0.0, 0.1),
     'L1_xattn_f2_b1': (0.0, 0.323),
     'L1_xattn_f2_b2': (0.0, 0.1)}
    factors = {'L1_xattn_sq_w': 8.0, 'L1_xattn_sk_w': 8.0, 'L1_xattn_cq_w': 8.0, 'L1_xattn_ck_w': 8.0}
    for name, (base, spread) in spreads.items():
        noise = np.random.default_rng([zlib.crc32(name.encode()), seed]).standard_normal(out[name].shape)
        drawn = base * np.exp(spread * noise) if base else spread * noise
        out[name] = jnp.asarray(drawn.astype(out[name].dtype))
    for name, factor in factors.items():
        out[name] = (out[name] * factor).astype(out[name].dtype)
    return out
```

```python
from contextlib import ExitStack

import concourse.bass as bass
from concourse import mybir

F32 = mybir.dt.float32
F32R = mybir.dt.float32r
ALU = mybir.AluOpType
ACT = mybir.ActivationFunctionType
AX = mybir.AxisListType

P = 128
B = 4
NQ = 512
DIM = 256
KT = DIM // P
CTX = 192
CP = CTX // 2
SC = 1601
SCP = SC + 1
HEADS = 16
FF = 1024
FT = FF // P
EPS = 1e-5
BANK = 512


class Attention:

    def __init__(self, name, layer, keys, cross):
        self.name, self.layer, self.keys, self.cross = name, layer, keys, cross
        self.dh = 64 if layer == 0 else 16
        self.G = 2 if layer == 0 else 4
        self.M = P // self.G
        self.inner = HEADS * self.dh
        self.groups_b = HEADS // self.G
        self.NG = B * self.groups_b
        self.kp = keys + keys % 2
        self.NC = -(-keys // P)
        self.NCP = -(-self.NC // 2)
        self.U = self.NCP * self.G
        self.scale = self.dh ** -0.5
        self.NB = -(-keys // BANK)
        self.blk = keys if self.NB == 1 else 402
        self.block_at = [0] if self.NB == 1 else [0, 400, 800, keys - 402]
        self.rows = self.inner // self.groups_b

    def chunk_rows(self, c):
        return min(P, self.keys - c * P)

    def pair(self, cp):
        return [c for c in (2 * cp, 2 * cp + 1) if c < self.NC]


SELF0 = Attention("self0", 0, NQ, False)
CROSS0 = Attention("cross0", 0, SC, True)
SELF1 = Attention("self1", 1, NQ, False)
CROSS1 = Attention("cross1", 1, SC, True)

VECTORS = [("L0_xattn_bo1", 2), ("L0_xattn_bo2", 2), ("L0_xattn_bp", 16), ("L0_xattn_bf", 2),
           ("L0_xattn_g1", 2), ("L0_xattn_b1", 2), ("L0_xattn_g2", 2), ("L0_xattn_b2", 2),
           ("L0_xattn_g3", 2), ("L0_xattn_b3", 2), ("L1_xattn_so_b", 2), ("L1_xattn_co_b", 2),
           ("L1_xattn_n1_g", 2), ("L1_xattn_n1_b", 2), ("L1_xattn_n2_g", 2), ("L1_xattn_n2_b", 2),
           ("L1_xattn_n3_g", 2), ("L1_xattn_n3_b", 2), ("L1_xattn_n4_g", 2), ("L1_xattn_n4_b", 2),
           ("L1_xattn_f1_b1", 8), ("L1_xattn_f1_b2", 2), ("L1_xattn_f2_b1", 8), ("L1_xattn_f2_b2", 2)]
VEC_AT, _n = {}, 0
for _name, _w in VECTORS:
    VEC_AT[_name] = _n
    _n += _w
NVEC = _n


def words(ap):
    return ap.bitcast(F32) if ap.dtype == F32R else ap


class Program:

    def __init__(self, nc, ins, out, keep):
        self.nc, self.ins, self.out, self.keep = nc, ins, out, keep
        self.phase_sems, self.old_sems, self.handles, self.old_handles = ExitStack(), ExitStack(), [], []

        def dram(name, shape, dt):
            return nc.dram_tensor(name, shape, dt, kind="Internal").ap()

        self.x = dram("x_scratch", [B, P, KT, NQ], F32)
        self.ctx_hi = dram("ctx_hi", [B, CP, 2, SCP], F32)
        self.ctx_lo = dram("ctx_lo", [B, CP, 2, SCP], F32)
        self.q, self.k, self.v, self.o = {}, {}, {}, {}
        for a in (SELF0, CROSS0, SELF1, CROSS1):
            self.q[a.name] = [dram(f"q_{p}_{a.name}", [a.NG, a.rows, NQ], F32) for p in ("hi", "lo")]
            self.k[a.name] = [dram(f"k_{p}_{a.name}", [a.NG, a.rows, a.kp], F32) for p in ("hi", "lo")]
            self.v[a.name] = dram(f"v_{a.name}", [a.NG, P, a.NC, P], F32)
            self.o[a.name] = [dram(f"o_{p}_{a.name}", [a.NG, P, NQ], F32) for p in ("hi", "lo")]
        self.vec = self.sbuf("vectors", [P, NVEC], F32)
        self.ones = self.sbuf("ones", [P, P], F32)
        self.mean_ones = self.sbuf("mean_ones", [P, P], F32)
        self.ident = self.sbuf("ident", [P, P], F32)
        self.den_sel = self.sbuf("den_sel", [P, P], F32)

    def sbuf(self, name, shape, dt):
        return self.keep.enter_context(self.nc.sbuf_tensor(name, shape, dt))

    def sem(self, name):
        handle = self.phase_sems.enter_context(self.nc.semaphore(name))
        self.handles.append(handle)
        return handle

    def start_phase(self):
        self.old_sems.close()
        self.old_sems, self.old_handles = self.phase_sems, self.handles
        self.phase_sems, self.handles = ExitStack(), []

    def clear_old(self, pool):
        for handle in self.old_handles:
            pool.sem_clear(handle)

    def vcol(self, name, t):
        at = VEC_AT[name] + t
        return self.vec[:, at:at + 1]


def setup_phase(pr):
    nc = pr.nc
    pr.start_phase()
    vec_loaded, const_step = pr.sem("vec_loaded"), pr.sem("const_step")
    ctx_loaded = [pr.sem(f"ctx_loaded{s}") for s in range(2)]
    hi_done, lo_done = pr.sem("ctx_hi_done"), pr.sem("ctx_lo_done")
    stored = [pr.sem(f"ctx_stored{s}") for s in range(2)]
    with ExitStack() as st:
        raw = st.enter_context(nc.sbuf_tensor("ctx_raw", [CP, 2, 2 * SCP], F32))
        hi = st.enter_context(nc.sbuf_tensor("ctx_hi_sb", [CP, 2, 2 * SCP], F32R))
        lo = st.enter_context(nc.sbuf_tensor("ctx_lo_sb", [CP, 2, 2 * SCP], F32R))
        block = st.enter_context(nc.Block())
        ctx_in = pr.ins["ctx"].rearrange("b p t s -> b p (t s)")
        ctx_out = [t.rearrange("b p t s -> b p (t s)") for t in (pr.ctx_hi, pr.ctx_lo)]

        @block.sync
        def _(sp):
            sp.dma_start(pr.vec[:], pr.ins["vec"]).then_inc(vec_loaded, 16)
            for b in range(2):
                sp.dma_start(raw[:, b, :], ctx_in[b]).then_inc(ctx_loaded[b], 16)
            for b in range(B):
                sp.wait_ge(lo_done, b + 1)
                sp.dma_start(ctx_out[0][b], words(hi[:, b % 2, :])).then_inc(stored[b % 2], 16)
                sp.dma_start(ctx_out[1][b], words(lo[:, b % 2, :])).then_inc(stored[b % 2], 16)
                if b + 2 < B:
                    sp.dma_start(raw[:, b % 2, :], ctx_in[b + 2]).then_inc(ctx_loaded[b % 2], 16)
            for s in range(2):
                sp.wait_ge(stored[s], 32 * (B // 2))
            sp.wait_ge(vec_loaded, 16)

        @block.gpsimd
        def _(pool):
            nc.gpsimd.memset(pr.ones[:], 1.0)
            nc.gpsimd.memset(pr.mean_ones[:], 1.0 / DIM)
            nc.gpsimd.memset(pr.ident[:], 0.0).then_inc(const_step, 1)
            nc.gpsimd.memset(pr.den_sel[:], 0.0).then_inc(const_step, 1)
            pool.wait_ge(const_step, 2)
            nc.gpsimd.affine_select(out=pr.ident[:], in_=pr.ident[:], compare_op=ALU.not_equal, fill=1.0,
                                    base=0, pattern=[[-1, P]], channel_multiplier=1).then_inc(const_step, 1)
            nc.gpsimd.affine_select(out=pr.den_sel[:].rearrange("p (h m) -> p h m", h=4),
                                    in_=pr.den_sel[:].rearrange("p (h m) -> p h m", h=4),
                                    compare_op=ALU.not_equal, fill=1.0, base=-16,
                                    pattern=[[-32, 4], [0, 32]], channel_multiplier=1).then_inc(const_step, 1)
            pool.wait_ge(const_step, 4)

        @block.scalar
        def _(act):
            for b in range(B):
                act.wait_ge(ctx_loaded[b % 2], 16 * (b // 2 + 1))
                if b >= 2:
                    act.wait_ge(stored[b % 2], 32 * (b // 2))
                nc.scalar.copy(hi[:, b % 2, :], raw[:, b % 2, :]).then_inc(hi_done, 1)

        @block.vector
        def _(dve):
            for b in range(B):
                dve.wait_ge(hi_done, b + 1)
                if b >= 2:
                    dve.wait_ge(stored[b % 2], 32 * (b // 2))
                nc.vector.tensor_tensor(lo[:, b % 2, :], raw[:, b % 2, :], hi[:, b % 2, :].bitcast(F32),
                                        ALU.subtract).then_inc(lo_done, 1)


def project_phase(pr, name, after=None, ff=None, attn=None, x_in=None, x_out=None):
    nc = pr.nc
    pr.start_phase()
    n_ln = (ff is not None) + (attn is not None)
    geglu = ff is not None and ff[0] == "geglu"
    a = attn[0] if attn else None
    qt = a.inner // P if attn else 0
    kcols = ([(0, NQ)] if not a.cross else [(0, 402), (402, 400), (802, 400), (1202, 400)]) if attn else []
    vhalf = a.inner // min(a.inner, BANK) if attn else 0
    vw = a.inner // vhalf if attn else 0

    at, ND = {}, 0
    for part, n in (("after", KT * bool(after)), ("ln_ff", 2 * bool(ff)), ("ff_a", FT * geglu),
                    ("ff_out", KT * bool(ff)), ("ln_attn", 2 * bool(attn)), ("q", qt), ("k", qt * len(kcols))):
        at[part] = ND
        ND += n
    N_GATE = FT if ff else 0
    NA = N_GATE + (a.NC * vhalf if attn else 0)
    x_final = (at["ff_out"] if ff else at["after"]) + KT
    NSPLIT = qt * (1 + len(kcols))
    NV = a.NC if attn else 0
    LN_DVE, LN_ACT = 3, 3
    uses = [(NSPLIT - s + 3) // 4 for s in range(4)]
    v_uses = [(NV - s + 1) // 2 for s in range(2)]

    def sem(what):
        return pr.sem(f"{name}_{what}")

    w_raw = [sem(f"w_raw{s}") for s in range(2)]
    w_hi, w_split = sem("w_hi"), sem("w_split")
    x_loaded, o_loaded, c_loaded, x_stored = sem("x_loaded"), sem("o_loaded"), sem("c_loaded"), sem("x_stored")
    d_tile, d_read, a_tile, a_read = sem("d_tile"), sem("d_read"), sem("a_tile"), sem("a_read")
    ln_dve, ln_act, u_hi, u_lo, hi_done = sem("ln_dve"), sem("ln_act"), sem("u_hi"), sem("u_lo"), sem("hi_done")
    split_stored = [sem(f"split_stored{s}") for s in range(4)]
    pad_done = sem("pad_done")
    v_stored = [sem(f"v_stored{s}") for s in range(2)]

    with ExitStack() as st:
        def sb(what, shape, dt=F32):
            return st.enter_context(nc.sbuf_tensor(f"{name}_{what}", shape, dt))

        weights = []

        def weight(which, p, t, n):
            pair = [sb(f"{which}_{h}", [p, t, n], F32R) for h in ("hi", "lo")]
            weights.append((which, pair[0], pair[1], p, t, n))
            return pair

        if after:
            ko = after[0].groups_b
            wo = weight(after[1], P, ko, DIM)
        if ff:
            w1 = weight(ff[3], P, KT, FF * (1 + geglu))
            w2 = weight(ff[5], P, FT, DIM)
        if attn:
            kp_, ktl = (CP, 2) if a.cross else (P, KT)
            wq = weight(attn[3], P, KT, a.inner)
            wk = weight(attn[4], kp_, ktl, a.inner)
            wv = weight(attn[5], kp_, ktl, a.inner)

        x = sb("x", [P, KT, NQ])
        if n_ln:
            xc, sq, ud = sb("xc", [P, KT, NQ]), sb("sq", [P, KT, NQ]), sb("ud", [P, KT, NQ])
            var, dev = sb("var", [P, NQ]), sb("dev", [P, NQ])
            z = [sb(f"z_{h}", [P, KT, NQ], F32R) for h in ("hi", "lo")]
        if after:
            o = [sb(f"o_{h}", [P, ko, NQ], F32R) for h in ("hi", "lo")]
        if ff:
            u = [sb(f"u_{h}", [P, FT, NQ], F32R) for h in ("hi", "lo")]
            gate = sb("gate", [P, 2, NQ])
            uf = sb("uf", [P, 2, NQ]) if geglu else gate
        if attn:
            sp_hi, sp_lo = sb("split_hi", [P, 4, NQ], F32R), sb("split_lo", [P, 4, NQ], F32R)
            v_sb = sb("v_sb", [P, 2, a.groups_b * P])
            if a.cross:
                c = [sb(f"c_{h}", [CP, 2, SCP], F32R) for h in ("hi", "lo")]
        wtmp = sb("w_tmp", [P, 2, 1024])
        ps = st.enter_context(nc.psum_tensor(f"{name}_ps", [P, 8, BANK], F32))
        block = st.enter_context(nc.Block())

        pieces = []
        for which, hi, lo, p, t, n in weights:
            src = pr.ins[which].rearrange("(t p) n -> p t n", p=p)
            step = max(1, 1024 // n)
            for t0 in range(0, t, step):
                for n0 in range(0, n, 1024):
                    n1 = min(n, n0 + 1024)
                    t1 = min(t, t0 + step)
                    pieces.append((src[:, t0:t1, n0:n1], hi[:, t0:t1, n0:n1], lo[:, t0:t1, n0:n1],
                                   p, t1 - t0, n1 - n0))

        def raw_piece(i):
            _, _, _, p, t, n = pieces[i]
            return wtmp[0:p, i % 2, 0:t * n].rearrange("p (t n) -> p t n", t=t)

        def product3(pe, out, w, wsl, y, ysl, kts, first=True):
            n = 0
            for kt in range(kts):
                for wi, yi in ((0, 0), (0, 1), (1, 0)):
                    last = nc.tensor.matmul(out, w[wi][(slice(None), kt) + wsl], y[yi][(slice(None), kt) + ysl],
                                            start=(n == 0), stop=(n == 3 * kts - 1))
                    n += 1
            return last

        @block.sync
        def _(sp):
            def load_x(b):
                sp.dma_start(x[:], x_in[bass.ds(b, 1)].rearrange("b p t n -> (b p) t n")).then_inc(x_loaded, 16)

            def load_o(b):
                for h in range(2):
                    sp.dma_start(words(o[h][:]), pr.o[after[0].name][h][bass.ds(b * ko, ko)]
                                 .rearrange("g p n -> p g n")).then_inc(o_loaded, 16)

            def load_context(b):
                for h, src in enumerate((pr.ctx_hi, pr.ctx_lo)):
                    sp.dma_start(words(c[h][:]), src[bass.ds(b, 1)].rearrange("b p t s -> (b p) t s"))\
                        .then_inc(c_loaded, 16)

            def rows_of(scr, b, m, c0, w):
                flat = scr.rearrange("(b g) r s -> b (g r) s", b=B)
                return flat[bass.ds(b, 1), m * P:(m + 1) * P, c0:c0 + w].rearrange("b r s -> (b r) s")

            def store_split(b, n, scr, m, c0, w):
                sp.wait_ge(d_read, b * ND + at["q"] + n + 1)
                for part, src in zip(scr, (sp_hi, sp_lo)):
                    sp.dma_start(rows_of(part, b, m, c0, w), words(src[:, n % 4, 0:w]))\
                        .then_inc(split_stored[n % 4], 16)

            def element(b, more):
                sp.wait_ge(d_read, b * ND + (at["ln_attn"] + 1 if attn else x_final))
                if x_out is not None:
                    sp.dma_start(x_out[bass.ds(b, 1)].rearrange("b p t n -> (b p) t n"), x[:])\
                        .then_inc(x_stored, 16)
                if more:
                    if after:
                        load_o(b + 1)
                    if x_out is not None:
                        sp.wait_ge(x_stored, 16 * (b + 1))
                    load_x(b + 1)
                if attn:
                    for m in range(qt):
                        store_split(b, m, pr.q[a.name], m, 0, NQ)
                    for m in range(qt):
                        for n, (c0, w) in enumerate(kcols):
                            store_split(b, qt + m * len(kcols) + n, pr.k[a.name], m, c0, w)
                    for ch in range(NV):
                        sp.wait_ge(a_read, b * NA + N_GATE + (ch + 1) * vhalf)
                        r = a.chunk_rows(ch)
                        dst = pr.v[a.name][bass.ds(b * a.groups_b, a.groups_b), 0:r, ch, :]
                        sp.dma_start(dst.rearrange("g p m -> p g m"),
                                     v_sb[0:r, ch % 2, :].rearrange("p (g m) -> p g m", m=P))\
                            .then_inc(v_stored[ch % 2], 16)
                    if more and a.cross:
                        load_context(b + 1)

            load_x(0)
            if after:
                load_o(0)
            if attn and a.cross:
                load_context(0)
            for i, piece in enumerate(pieces):
                if i >= 2:
                    sp.wait_ge(w_split, i - 1)
                sp.dma_start(raw_piece(i), piece[0]).then_inc(w_raw[i % 2], 16)
            with sp.Fori(0, B - 1, 1) as b:
                element(b, True)
            element(B - 1, False)
            if x_out is not None:
                sp.wait_ge(x_stored, 16 * B)
            if attn:
                for s in range(4):
                    if uses[s]:
                        sp.wait_ge(split_stored[s], 32 * B * uses[s])
                for s in range(2):
                    sp.wait_ge(v_stored[s], 16 * B * v_uses[s])

        @block.gpsimd
        def _(pool):
            pr.clear_old(pool)
            if attn and a.layer == 1:
                pad = v_sb[:].rearrange("p s (h m) -> p (s h) m", m=32)
                nc.gpsimd.memset(pad[:, :, 16:32], 0.0).then_inc(pad_done, 1)
                pool.wait_ge(pad_done, 1)
                nc.gpsimd.memset(pad[:, :, 16:17], 1.0).then_inc(pad_done, 1)

        @block.tensor
        def _(pe):
            pe.wait_ge(w_split, len(pieces))
            with pe.Fori(0, B, 1) as b:
                d = 0
                ac = 0

                def d_bank():
                    pe.wait_ge(d_read, b * ND + max(d - 3, 0))
                    return ps[:, d % 4, :]

                def a_bank():
                    pe.wait_ge(a_read, b * NA + max(ac - 3, 0))
                    return ps[:, 4 + ac % 4, :]

                ln = 0

                def mean_and_var():
                    nonlocal d, ln
                    base = (b * n_ln + ln) * LN_DVE
                    for what, src in ((0, x), (1, sq)):
                        if what:
                            pe.wait_ge(ln_act, (b * n_ln + ln) * LN_ACT + 1)
                        out = d_bank()
                        for kt in range(KT):
                            last = nc.tensor.matmul(out, pr.mean_ones[:], src[:, kt, :],
                                                    start=(kt == 0), stop=(kt == KT - 1))
                        last.then_inc(d_tile, 1)
                        d += 1
                    pe.wait_ge(ln_dve, base + LN_DVE)
                    ln += 1

                pe.wait_ge(x_loaded, 16 * (b + 1))
                if after:
                    pe.wait_ge(o_loaded, 32 * (b + 1))
                    for m in range(KT):
                        product3(pe, d_bank(), wo, (slice(m * P, (m + 1) * P),), o, (slice(None),), ko)\
                            .then_inc(d_tile, 1)
                        d += 1
                    pe.wait_ge(d_read, b * ND + d)
                if ff:
                    mean_and_var()
                    for m in range(FT):
                        g0 = FF * geglu + m * P
                        product3(pe, a_bank(), w1, (slice(g0, g0 + P),), z, (slice(None),), KT)\
                            .then_inc(a_tile, 1)
                        ac += 1
                        if geglu:
                            product3(pe, d_bank(), w1, (slice(m * P, (m + 1) * P),), z, (slice(None),), KT)\
                                .then_inc(d_tile, 1)
                            d += 1
                    pe.wait_ge(u_lo, (b + 1) * FT)
                    for m in range(KT):
                        product3(pe, d_bank(), w2, (slice(m * P, (m + 1) * P),), u, (slice(None),), FT)\
                            .then_inc(d_tile, 1)
                        d += 1
                    if attn:
                        pe.wait_ge(d_read, b * ND + d)
                if attn:
                    mean_and_var()
                    for m in range(qt):
                        product3(pe, d_bank(), wq, (slice(m * P, (m + 1) * P),), z, (slice(None),), KT)\
                            .then_inc(d_tile, 1)
                        d += 1
                    src, kts = (c, 2) if a.cross else (z, KT)
                    if a.cross:
                        pe.wait_ge(c_loaded, 32 * (b + 1))
                    for m in range(qt):
                        for c0, w in kcols:
                            product3(pe, d_bank()[:, 0:w], wk, (slice(m * P, (m + 1) * P),), src,
                                     (slice(c0, c0 + w),), kts).then_inc(d_tile, 1)
                            d += 1
                    for ch in range(NV):
                        r = a.chunk_rows(ch)
                        for hf in range(vhalf):
                            product3(pe, a_bank()[0:r, 0:vw], src, (slice(ch * P, ch * P + r),), wv,
                                     (slice(hf * vw, (hf + 1) * vw),), kts).then_inc(a_tile, 1)
                            ac += 1
                assert (d, ac) == (ND, NA)

        @block.scalar
        def _(act):
            for i in range(len(pieces)):
                act.wait_ge(w_raw[i % 2], 16 * (i // 2 + 1))
                nc.scalar.copy(pieces[i][1], raw_piece(i)).then_inc(w_hi, 1)
            with act.Fori(0, B, 1) as b:
                d = ac = ln = 0

                def layernorm_act(gain):
                    nonlocal d, ln
                    act.wait_ge(d_read, b * ND + d + 1)
                    nc.scalar.activation(sq[:], xc[:], ACT.Square).then_inc(ln_act, 1)
                    act.wait_ge(ln_dve, (b * n_ln + ln) * LN_DVE + 1)
                    nc.scalar.activation(dev[:], var[:], ACT.Sqrt).then_inc(ln_act, 1)
                    act.wait_ge(ln_dve, (b * n_ln + ln) * LN_DVE + 2)
                    for kt in range(KT):
                        last = nc.scalar.activation(z[0][:, kt, :], ud[:, kt, :], ACT.Identity,
                                                    bias=pr.vcol(gain[1], kt))
                    last.then_inc(ln_act, 1)
                    d += 2
                    ln += 1

                if after:
                    d += KT
                if ff:
                    layernorm_act(ff[1:3])
                    bias = ff[4]

                    def u_round(m):
                        if geglu:
                            act.wait_ge(d_read, b * ND + at["ff_a"] + m + 1)
                        else:
                            act.wait_ge(a_read, b * NA + m + 1)
                        nc.scalar.copy(u[0][:, m, :], uf[:, m % 2, :]).then_inc(u_hi, 1)

                    for m in range(FT):
                        act.wait_ge(a_tile, b * NA + ac + 1)
                        if geglu:
                            act.wait_ge(d_read, b * ND + at["ff_a"] + max(m - 1, 0))
                        else:
                            act.wait_ge(u_lo, b * FT + max(m - 1, 0))
                        done = nc.scalar.activation(gate[:, m % 2, :], ps[:, 4 + ac % 4, :], ACT.Gelu,
                                                    bias=pr.vcol(bias, FT * geglu + m))
                        done.then_inc(a_read, 1)
                        ac += 1
                        if geglu:
                            d += 1
                        if m:
                            u_round(m - 1)
                    u_round(FT - 1)
                    d += KT
                if attn:
                    layernorm_act(attn[1:3])
                    for m in range(NSPLIT):
                        w = NQ if m < qt else kcols[(m - qt) % len(kcols)][1]
                        act.wait_ge(d_tile, b * ND + d + 1)
                        act.wait_ge(split_stored[m % 4], 32 * (b * uses[m % 4] + m // 4))
                        nc.scalar.copy(sp_hi[:, m % 4, 0:w], ps[:, d % 4, 0:w]).then_inc(hi_done, 1)
                        d += 1
                    if a.layer == 1:
                        act.wait_ge(pad_done, 2)
                    for ch in range(NV):
                        r = a.chunk_rows(ch)
                        act.wait_ge(v_stored[ch % 2], 16 * (b * v_uses[ch % 2] + ch // 2))
                        for hf in range(vhalf):
                            act.wait_ge(a_tile, b * NA + ac + 1)
                            src = ps[0:r, 4 + ac % 4, 0:vw]
                            if a.layer == 0:
                                dst = v_sb[0:r, ch % 2, hf * vw:(hf + 1) * vw]
                            else:
                                dst = v_sb[0:r, ch % 2, :].rearrange("p (h m) -> p h m", m=32)[:, :, 0:16]
                                src = src.rearrange("p (h m) -> p h m", m=16)
                            nc.scalar.copy(dst, src).then_inc(a_read, 1)
                            ac += 1

        @block.vector
        def _(dve):
            for i in range(len(pieces)):
                dve.wait_ge(w_hi, i + 1)
                nc.vector.tensor_tensor(pieces[i][2], raw_piece(i), pieces[i][1].bitcast(F32), ALU.subtract)\
                    .then_inc(w_split, 1)
            with dve.Fori(0, B, 1) as b:
                d = ln = 0

                def next_tile():
                    dve.wait_ge(d_tile, b * ND + d + 1)
                    return ps[:, d % 4, :]

                def layernorm_dve(gain):
                    nonlocal d, ln
                    dbase, abase = (b * n_ln + ln) * LN_DVE, (b * n_ln + ln) * LN_ACT
                    mean = next_tile()
                    for kt in range(KT):
                        last = nc.vector.tensor_tensor(xc[:, kt, :], x[:, kt, :], mean, ALU.subtract)
                    last.then_inc(d_read, 1)
                    d += 1
                    nc.vector.tensor_scalar(var[:], next_tile(), EPS, None, ALU.add).then_inc(d_read, 1)
                    d += 1
                    dve.wait_ge(d_read, b * ND + d)
                    nc.vector.reciprocal(var[:], var[:]).then_inc(ln_dve, 1)
                    dve.wait_ge(ln_act, abase + 2)
                    for kt in range(KT):
                        last = nc.vector.scalar_tensor_tensor(
                            out=ud[:, kt, :], in0=xc[:, kt, :], scalar=pr.vcol(gain[0], kt), in1=dev[:],
                            op0=ALU.mult, op1=ALU.mult)
                    last.then_inc(ln_dve, 1)
                    dve.wait_ge(ln_act, abase + 3)
                    for kt in range(KT):
                        last = nc.vector.scalar_tensor_tensor(
                            out=z[1][:, kt, :], in0=ud[:, kt, :], scalar=pr.vcol(gain[1], kt),
                            in1=z[0][:, kt, :].bitcast(F32), op0=ALU.add, op1=ALU.subtract)
                    last.then_inc(ln_dve, 1)
                    ln += 1

                def residual(bias):
                    nonlocal d
                    for m in range(KT):
                        nc.vector.scalar_tensor_tensor(out=x[:, m, :], in0=next_tile(), scalar=pr.vcol(bias, m),
                                                       in1=x[:, m, :], op0=ALU.add, op1=ALU.add)\
                            .then_inc(d_read, 1)
                        d += 1
                    dve.wait_ge(d_read, b * ND + d)

                dve.wait_ge(x_loaded, 16 * (b + 1))
                if after:
                    residual(after[2])
                if ff:
                    layernorm_dve(ff[1:3])

                    def u_low(m):
                        dve.wait_ge(u_hi, b * FT + m + 1)
                        nc.vector.tensor_tensor(u[1][:, m, :], uf[:, m % 2, :], u[0][:, m, :].bitcast(F32),
                                                ALU.subtract).then_inc(u_lo, 1)

                    for m in range(FT):
                        if geglu:
                            t = next_tile()
                            dve.wait_ge(a_read, b * NA + m + 1)
                            dve.wait_ge(u_lo, b * FT + max(m - 1, 0))
                            nc.vector.scalar_tensor_tensor(
                                out=uf[:, m % 2, :], in0=t, scalar=pr.vcol(ff[4], m), in1=gate[:, m % 2, :],
                                op0=ALU.add, op1=ALU.mult).then_inc(d_read, 1)
                            d += 1
                        if m:
                            u_low(m - 1)
                    u_low(FT - 1)
                    residual(ff[6])
                if attn:
                    layernorm_dve(attn[1:3])
                    for m in range(NSPLIT):
                        w = NQ if m < qt else kcols[(m - qt) % len(kcols)][1]
                        t = next_tile()
                        dve.wait_ge(hi_done, b * NSPLIT + m + 1)
                        nc.vector.tensor_tensor(sp_lo[:, m % 4, 0:w], t[:, 0:w],
                                                sp_hi[:, m % 4, 0:w].bitcast(F32), ALU.subtract)\
                            .then_inc(d_read, 1)
                        d += 1


def attend_phase(pr, name, a):
    nc = pr.nc
    pr.start_phase()
    G, M, NC, NCP, U, NG, KP, NB, S = a.G, a.M, a.NC, a.NCP, a.U, a.NG, a.kp, a.NB, a.keys
    wide = a.layer == 0
    SLOTS = 3
    RC = 3
    IH = 4 * NB
    NI = IH * G
    NLOAD = (7 if wide else 9) + (NC * P > S)

    def items_until(u):
        return min(NI, -(-(u + 1) * NI // (U - 1)))

    row_at = [min(U - 1, next(u for u in range(U) if items_until(u) >= (h + 1) * IH) + 1) for h in range(G)]
    row_at[G - 1] = U
    FIN_U = 1 if wide else 2
    early_rows = sum(p < FIN_U for p in row_at)

    if NCP == 2:
        pool_sums, dve_sums = [(1, 0)], [(1, 1)]
    else:
        pool_sums = [(cp, h) for cp in (1, 2, 4, 5) for h in range(G)]
        dve_sums = [(cp, h) for cp in (3, 6) for h in range(G)]
    MERGE = G * (1 if NCP == 2 else 2)

    def sem(what):
        return pr.sem(f"{name}_{what}")

    loaded = [sem(f"loaded{r}") for r in range(SLOTS)]
    ones_set = sem("ones_set")
    item_done, item_read, max_done = sem("item_done"), sem("item_read"), sem("max_done")
    row_done, row_copied = sem("row_done"), sem("row_copied")
    st_done, exp_done, pv_done, pv_copied = sem("st_done"), sem("exp_done"), sem("pv_done"), sem("pv_copied")
    pool_sum, dve_sum, merged = sem("pool_sum"), sem("dve_sum"), sem("merged")
    den_done, den_read, divided = sem("den_done"), sem("den_read"), sem("divided")
    o_hi_done, o_lo_done = sem("o_hi_done"), sem("o_lo_done")
    o_stored = [sem(f"o_stored{s}") for s in range(SLOTS)]
    pv_read = divided if wide else pv_copied

    with ExitStack() as st:
        def sb(what, shape, dt=F32):
            return st.enter_context(nc.sbuf_tensor(f"{name}_{what}", shape, dt))

        KR = P if wide else 65
        kst = [sb(f"k_stack{r}", [KR, G, KP], F32R) for r in range(SLOTS)]
        qst = [sb(f"q_stack{r}", [KR, G, NQ], F32R) for r in range(SLOTS)]
        k2 = [sb(f"k_second{r}", [65, G, KP], F32R) for r in range(SLOTS)] if wide else kst
        q2 = [sb(f"q_second{r}", [65, G, NQ], F32R) for r in range(SLOTS)] if wide else qst
        v = [sb(f"v{r}", [P, NC, P]) for r in range(SLOTS)]
        prob = sb("prob", [P, RC, G, 2, BANK])
        blk_max = sb("blk_max", [P, SLOTS, G, 4, NB])
        row_max = sb("row_max", [P, SLOTS, G, 4, 1]) if NB > 1 else blk_max
        if wide:
            pool_acc, dve_acc = sb("pool_acc", [P, G, 2, BANK]), sb("dve_acc", [P, G, 2, BANK])
        inv_den = sb("inv_den", [P, NQ])
        if not wide:
            o_raw = sb("o_raw", [P, NQ])
        o_full = sb("o_full", [P, NQ])
        o_hi, o_lo = sb("o_hi", [P, SLOTS, NQ], F32R), sb("o_lo", [P, SLOTS, NQ], F32R)
        mx = st.enter_context(nc.psum_tensor(f"{name}_mx", [P, 2, BANK], F32))
        sc = st.enter_context(nc.psum_tensor(f"{name}_sc", [P, 2, 2, BANK], F32))
        pv = st.enter_context(nc.psum_tensor(f"{name}_pv", [P, BANK], F32))
        aux = st.enter_context(nc.psum_tensor(f"{name}_aux", [P, BANK], F32))
        block = st.enter_context(nc.Block())

        def prob_of(c, cp, h):
            return prob[:, (c * NCP + cp) % RC, h]

        def groups(eng, body, rounds):
            body(0, 0, True, False)
            with eng.Fori(0, rounds, 1) as q:
                for c in (1, 2, 3):
                    body(q, c, False, False)
            for i in range(1 + 3 * rounds, NG):
                body(i // 3, i % 3, False, i == NG - 1)

        LAST = ((NG - 1) // 3, (NG - 1) % 3)
        ROUNDS = (NG - 2) // 3

        @block.sync
        def _(sp):
            def load(q, c):
                r, one = c % 3, bass.ds(3 * q + c, 1)
                k_hi, k_lo = (t[one].rearrange("g (h r) s -> r (g h) s", h=G) for t in pr.k[a.name])
                q_hi, q_lo = (t[one].rearrange("g (h r) s -> r (g h) s", h=G) for t in pr.q[a.name])
                if wide:
                    moves = [(kst[r][0:64], k_hi), (kst[r][64:128], k_lo), (k2[r][0:64], k_hi),
                             (qst[r][0:64], q_hi), (qst[r][64:128], q_hi), (q2[r][0:64], q_lo)]
                else:
                    moves = [(kst[r][16 * n:16 * n + 16], (k_hi, k_lo)[n % 2]) for n in range(4)]
                    moves += [(qst[r][16 * n:16 * n + 16], (q_hi, q_lo)[n // 2]) for n in range(4)]
                vs = pr.v[a.name][one].rearrange("g p c m -> (g p) c m")
                full = S // P
                moves.append((v[r][:, 0:full, :], vs[:, 0:full, :]))
                if full < NC:
                    rows = a.chunk_rows(full)
                    moves.append((v[r][0:rows, full:NC, :], vs[0:rows, full:NC, :]))
                assert len(moves) == NLOAD
                for dst, src in moves:
                    sp.dma_start(words(dst), src).then_inc(loaded[r], 16)

            def store(q, c):
                r, i = c % 3, 3 * q + c
                sp.wait_ge(o_lo_done, i + 1)
                for dst, src in zip(pr.o[a.name], (o_hi, o_lo)):
                    sp.dma_start(dst[bass.ds(i, 1)].rearrange("i p n -> (i p) n"), words(src[:, r, :]))\
                        .then_inc(o_stored[r], 16)

            def main(q, c, first, more):
                if not first:
                    sp.wait_ge(pv_done, (3 * q + c) * NCP)
                if more:
                    load(q, c + 2)
                if not first:
                    store(q, c - 1)

            load(0, 0)
            load(0, 1)
            main(0, 0, True, True)
            rounds = (NG - 3) // 3
            with sp.Fori(0, rounds, 1) as q:
                for c in (1, 2, 3):
                    main(q, c, False, True)
            for i in range(1 + 3 * rounds, NG):
                main(i // 3, i % 3, False, i + 2 < NG)
            store(*LAST)
            for r in range(SLOTS):
                sp.wait_ge(o_stored[r], 32 * len(range(r, NG, SLOTS)))

        @block.gpsimd
        def _(pool):
            pr.clear_old(pool)
            for r in range(SLOTS):
                nc.gpsimd.memset(k2[r][64:65].bitcast(F32), 1.0).then_inc(ones_set, 1)

            def main(q, c, first, last):
                i = 3 * q + c
                for n, (cp, h) in enumerate(pool_sums):
                    pool.wait_ge(exp_done, i * U + cp * G + h + 1)
                    if cp == 1:
                        if not first:
                            pool.wait_ge(merged, i * MERGE)
                        other = prob_of(c, 0, h)
                    else:
                        pool.wait_ge(pool_sum, i * len(pool_sums) + n - G + 1)
                        other = pool_acc[:, h]
                    nc.gpsimd.tensor_tensor(pool_acc[:, h], prob_of(c, cp, h), other, ALU.add)\
                        .then_inc(pool_sum, 1)

            if wide:
                groups(pool, main, ROUNDS)

        @block.tensor
        def _(pe):
            def items(q, c, done, until):
                r, i = c % 3, 3 * q + c
                if done == 0:
                    pe.wait_ge(loaded[r], 16 * NLOAD * (q + c // 3 + 1))
                rows = KR if wide else 64
                for n in range(done, until):
                    h, t, at = n // IH, n % IH // NB, a.block_at[n % NB]
                    if not (isinstance(i, int) and i == 0 and n < 2):
                        pe.wait_ge(item_read, i * NI + n - 1)
                    nc.tensor.matmul(mx[:, n % 2, 0:a.blk], qst[r][0:rows, h, t * P:(t + 1) * P],
                                     kst[r][0:rows, h, at:at + a.blk], start=True, stop=True)\
                        .then_inc(item_done, 1)

            def row(q, c, h, dens):
                r, i = c % 3, 3 * q + c
                if NB > 1:
                    pe.wait_ge(max_done, i * G + h + 1)
                else:
                    pe.wait_ge(item_read, i * NI + (h + 1) * IH)
                pe.wait_ge(row_copied, i * G + h)
                pe.wait_ge(den_read, dens)
                for t in range(4):
                    last = nc.tensor.transpose(aux[0:1, t * P:(t + 1) * P], row_max[:, r, h, t], pr.ident[:])
                last.then_inc(row_done, 1)

            def scores(q, c, u, first):
                r, i, cp, h = c % 3, 3 * q + c, u // G, u % G
                if cp == 0:
                    pe.wait_ge(row_copied, i * G + h + 1)
                if not (first and u < 2):
                    pe.wait_ge(exp_done, i * U + u - 1)
                for ch in a.pair(cp):
                    rows, k0 = a.chunk_rows(ch), ch * P
                    out = sc[0:rows, u % 2, ch % 2, :]
                    if wide:
                        nc.tensor.matmul(out, kst[r][:, h, k0:k0 + rows], qst[r][:, h, :],
                                         start=True, stop=False)
                    last = nc.tensor.matmul(out, k2[r][0:65, h, k0:k0 + rows], q2[r][0:65, h, :],
                                            start=not wide, stop=True)
                last.then_inc(st_done, 1)

            def values(q, c, cp, first):
                r, i = c % 3, 3 * q + c
                pe.wait_ge(exp_done, i * U + (cp + 1) * G)
                if cp == 0 and not first:
                    pe.wait_ge(pv_read, i)
                for ch in a.pair(cp):
                    rows = a.chunk_rows(ch)
                    for h in range(G):
                        last = nc.tensor.matmul(pv[h * M:(h + 1) * M, :], v[r][0:rows, ch, h * M:(h + 1) * M],
                                                prob_of(c, cp, h)[0:rows, ch % 2, :],
                                                start=(ch == 0), stop=(ch == NC - 1))
                last.then_inc(pv_done, 1)

            def denominators(q, c, rows_before):
                i = 3 * q + c
                pe.wait_ge(row_copied, rows_before)
                if wide:
                    pe.wait_ge(merged, (i + 1) * MERGE)
                    for h in range(G):
                        last = nc.tensor.matmul(aux[h * M:(h + 1) * M, :], pr.ones[:, 0:M],
                                                dve_acc[:, h, 0, :], start=True, stop=True)
                else:
                    pe.wait_ge(pv_copied, i + 1)
                    last = nc.tensor.matmul(aux[:], pr.den_sel[:], o_raw[:], start=True, stop=True)
                last.then_inc(den_done, 1)

            def main(q, c, first, last):
                i = 3 * q + c
                row(q, c, G - 1, 0 if first else i - 1)
                done = 0
                for u in range(U):
                    scores(q, c, u, first)
                    if u == 0 and not first:
                        values(q, c - 1, NCP - 1, False)
                    if u == FIN_U and not first:
                        denominators(q, c - 1, (i + 1) * G + (0 if last else early_rows))
                    if not last:
                        items(q, c + 1, done, items_until(u))
                        done = items_until(u)
                        for h in range(G):
                            if row_at[h] == u:
                                row(q, c + 1, h, 0 if first else i if u >= FIN_U else i - 1)
                    if u % G == 0 and u > 0:
                        values(q, c, u // G - 1, first)

            pe.wait_ge(ones_set, SLOTS)
            items(0, 0, 0, NI)
            for h in range(G - 1):
                row(0, 0, h, 0)
            groups(pe, main, ROUNDS)
            values(*LAST, NCP - 1, False)
            denominators(*LAST, NG * G)

        @block.scalar
        def _(act):
            def row_copy(q, c, h):
                r, i = c % 3, 3 * q + c
                act.wait_ge(row_done, i * G + h + 1)
                nc.scalar.activation(q2[r][64:65, h, :], aux[0:1, :], ACT.Copy, scale=-1.0)\
                    .then_inc(row_copied, 1)

            def exps(q, c, u, first):
                i, cp, h = 3 * q + c, u // G, u % G
                act.wait_ge(st_done, i * U + u + 1)
                back, cpb = (cp - RC) // NCP, (cp - RC) % NCP
                if not (first and back < 0):
                    act.wait_ge(pv_done, i * NCP + cp - RC + 1)
                    if wide and back < -1:
                        act.wait_ge(merged, (i - 1) * MERGE)
                    elif wide:
                        unit = (max(cpb, 1), h)
                        if unit in pool_sums:
                            act.wait_ge(pool_sum, (i + back) * len(pool_sums) + pool_sums.index(unit) + 1)
                        else:
                            act.wait_ge(dve_sum, (i + back) * len(dve_sums) + dve_sums.index(unit) + 1)
                n, rows = len(a.pair(cp)), a.chunk_rows(2 * cp)
                nc.scalar.activation(prob_of(c, cp, h)[0:rows, 0:n, :], sc[0:rows, u % 2, 0:n, :], ACT.Exp,
                                     scale=a.scale).then_inc(exp_done, 1)

            def raw_copy(q, c):
                i = 3 * q + c
                act.wait_ge(divided, i)
                act.wait_ge(pv_done, (i + 1) * NCP)
                nc.scalar.copy(o_raw[:], pv[:]).then_inc(pv_copied, 1)

            def high_part(q, c):
                i = 3 * q + c
                act.wait_ge(divided, i + 1)
                act.wait_ge(o_stored[c % 3], 32 * (q + c // 3))
                nc.scalar.copy(o_hi[:, c % 3, :], o_full[:]).then_inc(o_hi_done, 1)

            def main(q, c, first, last):
                row_copy(q, c, G - 1)
                for u in range(U):
                    exps(q, c, u, first)
                    if u == 1 and not first and not wide:
                        raw_copy(q, c - 1)
                    if u == FIN_U + 1 and not first:
                        high_part(q, c - 1)
                    if not last:
                        for h in range(G):
                            if row_at[h] == u:
                                row_copy(q, c + 1, h)

            for h in range(G - 1):
                row_copy(0, 0, h)
            groups(act, main, ROUNDS)
            if not wide:
                raw_copy(*LAST)
            high_part(*LAST)

        @block.vector
        def _(dve):
            def items(q, c, done, until):
                r, i = c % 3, 3 * q + c
                for n in range(done, until):
                    h, t, nb = n // IH, n % IH // NB, n % NB
                    dve.wait_ge(item_done, i * NI + n + 1)
                    nc.vector.reduce_max(blk_max[:, r, h, t, nb:nb + 1], mx[:, n % 2, 0:a.blk], AX.X)\
                        .then_inc(item_read, 1)
                    if NB > 1 and n % IH == IH - 1:
                        dve.wait_ge(item_read, i * NI + n + 1)
                        nc.vector.reduce_max(row_max[:, r, h, :, 0], blk_max[:, r, h], AX.X)\
                            .then_inc(max_done, 1)

            def sums(q, c, cp, h):
                i, n = 3 * q + c, dve_sums.index((cp, h))
                acc = dve_acc[:, h]
                dve.wait_ge(exp_done, i * U + cp * G + h + 1)
                if cp <= 3:
                    dve.wait_ge(den_done, i)
                if cp == 1:
                    nc.vector.tensor_tensor(acc, prob_of(c, 0, h), prob_of(c, 1, h), ALU.add)\
                        .then_inc(dve_sum, 1)
                elif cp == 3:
                    nc.vector.tensor_copy(acc, prob_of(c, 3, h)).then_inc(dve_sum, 1)
                else:
                    rows = a.chunk_rows(2 * cp)
                    dve.wait_ge(dve_sum, i * len(dve_sums) + n - G + 1)
                    nc.vector.tensor_tensor(acc[0:rows, 0, :], acc[0:rows, 0, :],
                                            prob_of(c, cp, h)[0:rows, 0, :], ALU.add).then_inc(dve_sum, 1)

            def merge(q, c):
                i = 3 * q + c
                dve.wait_ge(pool_sum, (i + 1) * len(pool_sums))
                dve.wait_ge(dve_sum, (i + 1) * len(dve_sums))
                if NCP > 2:
                    for h in range(G):
                        nc.vector.tensor_tensor(dve_acc[:, h], dve_acc[:, h], pool_acc[:, h], ALU.add)\
                            .then_inc(merged, 1)
                    dve.wait_ge(merged, i * MERGE + G)
                for h in range(G):
                    acc = pool_acc[:, h] if (1, h) in pool_sums and NCP == 2 else dve_acc[:, h]
                    nc.vector.tensor_tensor(dve_acc[:, h, 0, :], acc[:, 0, :], acc[:, 1, :], ALU.add)\
                        .then_inc(merged, 1)

            def divide(q, c):
                i = 3 * q + c
                dve.wait_ge(den_done, i + 1)
                nc.vector.reciprocal(inv_den[:], aux[:]).then_inc(den_read, 1)
                dve.wait_ge(den_read, i + 1)
                dve.wait_ge(pv_done, (i + 1) * NCP)
                nc.vector.tensor_tensor(o_full[:], pv[:] if wide else o_raw[:], inv_den[:], ALU.mult)\
                    .then_inc(divided, 1)

            def low_part(q, c):
                i = 3 * q + c
                dve.wait_ge(o_hi_done, i + 1)
                nc.vector.tensor_tensor(o_lo[:, c % 3, :], o_full[:], o_hi[:, c % 3, :].bitcast(F32),
                                        ALU.subtract).then_inc(o_lo_done, 1)

            def main(q, c, first, last):
                done = 0
                for u in range(U):
                    if wide and u == 0 and not first:
                        sums(q, c - 1, NCP - 1, G - 1)
                        merge(q, c - 1)
                    if wide and u > 0 and ((u - 1) // G, (u - 1) % G) in dve_sums:
                        sums(q, c, (u - 1) // G, (u - 1) % G)
                    if not last:
                        items(q, c + 1, done, items_until(u))
                        done = items_until(u)
                    if u == FIN_U and not first:
                        divide(q, c - 1)
                    if u == FIN_U + 2 and not first:
                        low_part(q, c - 1)

            items(0, 0, 0, NI)
            groups(dve, main, ROUNDS)
            if wide:
                sums(*LAST, NCP - 1, G - 1)
                merge(*LAST)
            divide(*LAST)
            low_part(*LAST)


def build(nc, ins, out):
    with ExitStack() as keep:
        pr = Program(nc, ins, out, keep)
        w0, w1 = "L0_xattn_", "L1_xattn_"
        setup_phase(pr)
        project_phase(pr, "p0", x_in=ins["x"],
                      attn=(SELF0, w0 + "g1", w0 + "b1", w0 + "Wq1", w0 + "Wk1", w0 + "Wv1"))
        attend_phase(pr, "a0", SELF0)
        project_phase(pr, "p1", x_in=ins["x"], x_out=pr.x, after=(SELF0, w0 + "Wo1", w0 + "bo1"),
                      attn=(CROSS0, w0 + "g2", w0 + "b2", w0 + "Wq2", w0 + "Wk2", w0 + "Wv2"))
        attend_phase(pr, "a1", CROSS0)
        project_phase(pr, "p2", x_in=pr.x, x_out=pr.x, after=(CROSS0, w0 + "Wo2", w0 + "bo2"),
                      ff=("geglu", w0 + "g3", w0 + "b3", w0 + "Wp", w0 + "bp", w0 + "Wf", w0 + "bf"),
                      attn=(SELF1, w1 + "n1_g", w1 + "n1_b", w1 + "sq_w", w1 + "sk_w", w1 + "sv_w"))
        attend_phase(pr, "a2", SELF1)
        project_phase(pr, "p3", x_in=pr.x, x_out=pr.x, after=(SELF1, w1 + "so_w", w1 + "so_b"),
                      ff=("gelu", w1 + "n2_g", w1 + "n2_b", w1 + "f1_w1", w1 + "f1_b1", w1 + "f1_w2", w1 + "f1_b2"),
                      attn=(CROSS1, w1 + "n3_g", w1 + "n3_b", w1 + "cq_w", w1 + "ck_w", w1 + "cv_w"))
        attend_phase(pr, "a3", CROSS1)
        project_phase(pr, "p4", x_in=pr.x, x_out=out, after=(CROSS1, w1 + "co_w", w1 + "co_b"),
                      ff=("gelu", w1 + "n4_g", w1 + "n4_b", w1 + "f2_w1", w1 + "f2_b1", w1 + "f2_w2", w1 + "f2_b2"))


_WEIGHTS = (["L0_xattn_" + w for w in ("Wq1", "Wk1", "Wv1", "Wo1", "Wq2", "Wk2", "Wv2", "Wo2", "Wp", "Wf")]
            + ["L1_xattn_" + w for w in ("sq_w", "sk_w", "sv_w", "so_w", "cq_w", "ck_w", "cv_w", "co_w",
                                         "f1_w1", "f1_w2", "f2_w1", "f2_w2")])


def kernel(**inputs):
    import numpy as _np
    import concourse.bacc as _bacc
    from concourse import mybir as _mybir
    from concourse.bass_utils import run_bass_kernel_spmd as _run

    arr = {k: _np.asarray(v) for k, v in inputs.items()}

    def feature_major(t, p):
        return _np.ascontiguousarray(t.reshape(B, t.shape[1], -1, p).transpose(0, 3, 2, 1))

    arrays = {"x": feature_major(arr["x"], P)}
    ctx = _np.zeros((B, SCP, CTX), arr["ctx_768"].dtype)
    ctx[:, :SC] = arr["ctx_768"]
    arrays["ctx"] = feature_major(ctx, CP)
    arrays["vec"] = _np.ascontiguousarray(
        _np.concatenate([arr[n].reshape(w, P) for n, w in VECTORS]).T)
    for n in _WEIGHTS:
        w = arr[n]
        if n in ("L1_xattn_so_w", "L1_xattn_co_w"):
            wide = _np.zeros((HEADS, 32, DIM), w.dtype)
            wide[:, :16] = w.reshape(HEADS, 16, DIM)
            w = wide.reshape(HEADS * 32, DIM)
        arrays[n] = _np.ascontiguousarray(w)

    nc = _bacc.Bacc("TRN2", target_bir_lowering=False, num_devices=1)
    ins = {n: nc.dram_tensor(n + "_in", t.shape, _mybir.dt.from_np(t.dtype), kind="ExternalInput").ap()
           for n, t in arrays.items()}
    out = nc.dram_tensor("out_x", (B, P, KT, NQ), F32, kind="ExternalOutput").ap()
    build(nc, ins, out)
    r = _run(nc, [{n + "_in": t for n, t in arrays.items()}], core_ids=[0])
    got = r.results[0]["out_x"]
    return _np.ascontiguousarray(got.transpose(0, 3, 2, 1).reshape(B, NQ, DIM))
```

```python
from contextlib import ExitStack

import concourse.bass as bass
from concourse import mybir

F32 = mybir.dt.float32
F32R = mybir.dt.float32r
ALU = mybir.AluOpType
ACT = mybir.ActivationFunctionType
AX = mybir.AxisListType

P = 128
B = 4
NQ = 512
DIM = 256
KT = DIM // P
CTX = 192
CP = CTX // 2
SC = 1601
SCP = SC + 1
HEADS = 16
FF = 1024
FT = FF // P
EPS = 1e-5
BANK = 512


class Attention:

    def __init__(self, name, layer, keys, cross):
        self.name, self.layer, self.keys, self.cross = name, layer, keys, cross
        self.dh = 64 if layer == 0 else 16
        self.G = 2 if layer == 0 else 4
        self.M = P // self.G
        self.inner = HEADS * self.dh
        self.groups_b = HEADS // self.G
        self.NG = B * self.groups_b
        self.kp = keys + keys % 2
        self.NC = -(-keys // P)
        self.NCP = -(-self.NC // 2)
        self.U = self.NCP * self.G
        self.scale = self.dh ** -0.5
        self.NB = -(-keys // BANK)
        self.blk = keys if self.NB == 1 else 402
        self.block_at = [0] if self.NB == 1 else [0, 400, 800, keys - 402]
        self.rows = self.inner // self.groups_b

    def chunk_rows(self, c):
        return min(P, self.keys - c * P)

    def pair(self, cp):
        return [c for c in (2 * cp, 2 * cp + 1) if c < self.NC]


SELF0 = Attention("self0", 0, NQ, False)
CROSS0 = Attention("cross0", 0, SC, True)
SELF1 = Attention("self1", 1, NQ, False)
CROSS1 = Attention("cross1", 1, SC, True)

VECTORS = [("L0_xattn_bo1", 2), ("L0_xattn_bo2", 2), ("L0_xattn_bp", 16), ("L0_xattn_bf", 2),
           ("L0_xattn_g1", 2), ("L0_xattn_b1", 2), ("L0_xattn_g2", 2), ("L0_xattn_b2", 2),
           ("L0_xattn_g3", 2), ("L0_xattn_b3", 2), ("L1_xattn_so_b", 2), ("L1_xattn_co_b", 2),
           ("L1_xattn_n1_g", 2), ("L1_xattn_n1_b", 2), ("L1_xattn_n2_g", 2), ("L1_xattn_n2_b", 2),
           ("L1_xattn_n3_g", 2), ("L1_xattn_n3_b", 2), ("L1_xattn_n4_g", 2), ("L1_xattn_n4_b", 2),
           ("L1_xattn_f1_b1", 8), ("L1_xattn_f1_b2", 2), ("L1_xattn_f2_b1", 8), ("L1_xattn_f2_b2", 2)]
VEC_AT, _n = {}, 0
for _name, _w in VECTORS:
    VEC_AT[_name] = _n
    _n += _w
NVEC = _n


def words(ap):
    return ap.bitcast(F32) if ap.dtype == F32R else ap


class Program:

    def __init__(self, nc, ins, out, keep):
        self.nc, self.ins, self.out, self.keep = nc, ins, out, keep
        self.phase_sems, self.old_sems, self.handles, self.old_handles = ExitStack(), ExitStack(), [], []

        def dram(name, shape, dt):
            return nc.dram_tensor(name, shape, dt, kind="Internal").ap()

        self.x = dram("x_scratch", [B, P, KT, NQ], F32)
        self.ctx_hi = dram("ctx_hi", [B, CP, 2, SCP], F32)
        self.ctx_lo = dram("ctx_lo", [B, CP, 2, SCP], F32)
        self.q, self.k, self.v, self.o = {}, {}, {}, {}
        for a in (SELF0, CROSS0, SELF1, CROSS1):
            self.q[a.name] = [dram(f"q_{p}_{a.name}", [a.NG, a.rows, NQ], F32) for p in ("hi", "lo")]
            self.k[a.name] = [dram(f"k_{p}_{a.name}", [a.NG, a.rows, a.kp], F32) for p in ("hi", "lo")]
            self.v[a.name] = dram(f"v_{a.name}", [a.NG, P, a.NC, P], F32)
            self.o[a.name] = [dram(f"o_{p}_{a.name}", [a.NG, P, NQ], F32) for p in ("hi", "lo")]
        self.vec = self.sbuf("vectors", [P, NVEC], F32)
        self.ones = self.sbuf("ones", [P, P], F32)
        self.mean_ones = self.sbuf("mean_ones", [P, P], F32)
        self.ident = self.sbuf("ident", [P, P], F32)
        self.den_sel = self.sbuf("den_sel", [P, P], F32)

    def sbuf(self, name, shape, dt):
        return self.keep.enter_context(self.nc.sbuf_tensor(name, shape, dt))

    def sem(self, name):
        handle = self.phase_sems.enter_context(self.nc.semaphore(name))
        self.handles.append(handle)
        return handle

    def start_phase(self):
        self.old_sems.close()
        self.old_sems, self.old_handles = self.phase_sems, self.handles
        self.phase_sems, self.handles = ExitStack(), []

    def clear_old(self, pool):
        for handle in self.old_handles:
            pool.sem_clear(handle)

    def vcol(self, name, t):
        at = VEC_AT[name] + t
        return self.vec[:, at:at + 1]


def setup_phase(pr):
    nc = pr.nc
    pr.start_phase()
    vec_loaded, const_step = pr.sem("vec_loaded"), pr.sem("const_step")
    ctx_loaded = [pr.sem(f"ctx_loaded{s}") for s in range(2)]
    hi_done, lo_done = pr.sem("ctx_hi_done"), pr.sem("ctx_lo_done")
    stored = [pr.sem(f"ctx_stored{s}") for s in range(2)]
    with ExitStack() as st:
        raw = st.enter_context(nc.sbuf_tensor("ctx_raw", [CP, 2, 2 * SCP], F32))
        hi = st.enter_context(nc.sbuf_tensor("ctx_hi_sb", [CP, 2, 2 * SCP], F32R))
        lo = st.enter_context(nc.sbuf_tensor("ctx_lo_sb", [CP, 2, 2 * SCP], F32R))
        block = st.enter_context(nc.Block())
        ctx_in = pr.ins["ctx"].rearrange("b p t s -> b p (t s)")
        ctx_out = [t.rearrange("b p t s -> b p (t s)") for t in (pr.ctx_hi, pr.ctx_lo)]

        @block.sync
        def _(sp):
            sp.dma_start(pr.vec[:], pr.ins["vec"]).then_inc(vec_loaded, 16)
            for b in range(2):
                sp.dma_start(raw[:, b, :], ctx_in[b]).then_inc(ctx_loaded[b], 16)
            for b in range(B):
                sp.wait_ge(lo_done, b + 1)
                sp.dma_start(ctx_out[0][b], words(hi[:, b % 2, :])).then_inc(stored[b % 2], 16)
                sp.dma_start(ctx_out[1][b], words(lo[:, b % 2, :])).then_inc(stored[b % 2], 16)
                if b + 2 < B:
                    sp.dma_start(raw[:, b % 2, :], ctx_in[b + 2]).then_inc(ctx_loaded[b % 2], 16)
            for s in range(2):
                sp.wait_ge(stored[s], 32 * (B // 2))
            sp.wait_ge(vec_loaded, 16)

        @block.gpsimd
        def _(pool):
            nc.gpsimd.memset(pr.ones[:], 1.0)
            nc.gpsimd.memset(pr.mean_ones[:], 1.0 / DIM)
            nc.gpsimd.memset(pr.ident[:], 0.0).then_inc(const_step, 1)
            nc.gpsimd.memset(pr.den_sel[:], 0.0).then_inc(const_step, 1)
            pool.wait_ge(const_step, 2)
            nc.gpsimd.affine_select(out=pr.ident[:], in_=pr.ident[:], compare_op=ALU.not_equal, fill=1.0,
                                    base=0, pattern=[[-1, P]], channel_multiplier=1).then_inc(const_step, 1)
            nc.gpsimd.affine_select(out=pr.den_sel[:].rearrange("p (h m) -> p h m", h=4),
                                    in_=pr.den_sel[:].rearrange("p (h m) -> p h m", h=4),
                                    compare_op=ALU.not_equal, fill=1.0, base=-16,
                                    pattern=[[-32, 4], [0, 32]], channel_multiplier=1).then_inc(const_step, 1)
            pool.wait_ge(const_step, 4)

        @block.scalar
        def _(act):
            for b in range(B):
                act.wait_ge(ctx_loaded[b % 2], 16 * (b // 2 + 1))
                if b >= 2:
                    act.wait_ge(stored[b % 2], 32 * (b // 2))
                nc.scalar.copy(hi[:, b % 2, :], raw[:, b % 2, :]).then_inc(hi_done, 1)

        @block.vector
        def _(dve):
            for b in range(B):
                dve.wait_ge(hi_done, b + 1)
                if b >= 2:
                    dve.wait_ge(stored[b % 2], 32 * (b // 2))
                nc.vector.tensor_tensor(lo[:, b % 2, :], raw[:, b % 2, :], hi[:, b % 2, :].bitcast(F32),
                                        ALU.subtract).then_inc(lo_done, 1)


def project_phase(pr, name, after=None, ff=None, attn=None, x_in=None, x_out=None):
    nc = pr.nc
    pr.start_phase()
    n_ln = (ff is not None) + (attn is not None)
    geglu = ff is not None and ff[0] == "geglu"
    a = attn[0] if attn else None
    qt = a.inner // P if attn else 0
    kcols = ([(0, NQ)] if not a.cross else [(0, 402), (402, 400), (802, 400), (1202, 400)]) if attn else []
    vhalf = a.inner // min(a.inner, BANK) if attn else 0
    vw = a.inner // vhalf if attn else 0

    at, ND = {}, 0
    for part, n in (("after", KT * bool(after)), ("ln_ff", 2 * bool(ff)), ("ff_a", FT * geglu),
                    ("ff_out", KT * bool(ff)), ("ln_attn", 2 * bool(attn)), ("q", qt), ("k", qt * len(kcols))):
        at[part] = ND
        ND += n
    N_GATE = FT if ff else 0
    NA = N_GATE + (a.NC * vhalf if attn else 0)
    x_final = (at["ff_out"] if ff else at["after"]) + KT
    NSPLIT = qt * (1 + len(kcols))
    NV = a.NC if attn else 0
    LN_DVE, LN_ACT = 3, 3
    uses = [(NSPLIT - s + 3) // 4 for s in range(4)]
    v_uses = [(NV - s + 1) // 2 for s in range(2)]

    def sem(what):
        return pr.sem(f"{name}_{what}")

    w_raw = [sem(f"w_raw{s}") for s in range(2)]
    w_hi, w_split = sem("w_hi"), sem("w_split")
    x_loaded, o_loaded, c_loaded, x_stored = sem("x_loaded"), sem("o_loaded"), sem("c_loaded"), sem("x_stored")
    d_tile, d_read, a_tile, a_read = sem("d_tile"), sem("d_read"), sem("a_tile"), sem("a_read")
    ln_dve, ln_act, u_hi, u_lo, hi_done = sem("ln_dve"), sem("ln_act"), sem("u_hi"), sem("u_lo"), sem("hi_done")
    split_stored = [sem(f"split_stored{s}") for s in range(4)]
    pad_done = sem("pad_done")
    v_stored = [sem(f"v_stored{s}") for s in range(2)]

    with ExitStack() as st:
        def sb(what, shape, dt=F32):
            return st.enter_context(nc.sbuf_tensor(f"{name}_{what}", shape, dt))

        weights = []

        def weight(which, p, t, n):
            pair = [sb(f"{which}_{h}", [p, t, n], F32R) for h in ("hi", "lo")]
            weights.append((which, pair[0], pair[1], p, t, n))
            return pair

        if after:
            ko = after[0].groups_b
            wo = weight(after[1], P, ko, DIM)
        if ff:
            w1 = weight(ff[3], P, KT, FF * (1 + geglu))
            w2 = weight(ff[5], P, FT, DIM)
        if attn:
            kp_, ktl = (CP, 2) if a.cross else (P, KT)
            wq = weight(attn[3], P, KT, a.inner)
            wk = weight(attn[4], kp_, ktl, a.inner)
            wv = weight(attn[5], kp_, ktl, a.inner)

        x = sb("x", [P, KT, NQ])
        if n_ln:
            xc, sq, ud = sb("xc", [P, KT, NQ]), sb("sq", [P, KT, NQ]), sb("ud", [P, KT, NQ])
            var, dev = sb("var", [P, NQ]), sb("dev", [P, NQ])
            z = [sb(f"z_{h}", [P, KT, NQ], F32R) for h in ("hi", "lo")]
        if after:
            o = [sb(f"o_{h}", [P, ko, NQ], F32R) for h in ("hi", "lo")]
        if ff:
            u = [sb(f"u_{h}", [P, FT, NQ], F32R) for h in ("hi", "lo")]
            gate = sb("gate", [P, 2, NQ])
            uf = sb("uf", [P, 2, NQ]) if geglu else gate
        if attn:
            sp_hi, sp_lo = sb("split_hi", [P, 4, NQ], F32R), sb("split_lo", [P, 4, NQ], F32R)
            v_sb = sb("v_sb", [P, 2, a.groups_b * P])
            if a.cross:
                c = [sb(f"c_{h}", [CP, 2, SCP], F32R) for h in ("hi", "lo")]
        wtmp = sb("w_tmp", [P, 2, 1024])
        ps = st.enter_context(nc.psum_tensor(f"{name}_ps", [P, 8, BANK], F32))
        block = st.enter_context(nc.Block())

        pieces = []
        for which, hi, lo, p, t, n in weights:
            src = pr.ins[which].rearrange("(t p) n -> p t n", p=p)
            step = max(1, 1024 // n)
            for t0 in range(0, t, step):
                for n0 in range(0, n, 1024):
                    n1 = min(n, n0 + 1024)
                    t1 = min(t, t0 + step)
                    pieces.append((src[:, t0:t1, n0:n1], hi[:, t0:t1, n0:n1], lo[:, t0:t1, n0:n1],
                                   p, t1 - t0, n1 - n0))

        def raw_piece(i):
            _, _, _, p, t, n = pieces[i]
            return wtmp[0:p, i % 2, 0:t * n].rearrange("p (t n) -> p t n", t=t)

        def product3(pe, out, w, wsl, y, ysl, kts, first=True):
            n = 0
            for kt in range(kts):
                for wi, yi in ((0, 0), (0, 1), (1, 0)):
                    last = nc.tensor.matmul(out, w[wi][(slice(None), kt) + wsl], y[yi][(slice(None), kt) + ysl],
                                            start=(n == 0), stop=(n == 3 * kts - 1))
                    n += 1
            return last

        @block.sync
        def _(sp):
            def load_x(b):
                sp.dma_start(x[:], x_in[bass.ds(b, 1)].rearrange("b p t n -> (b p) t n")).then_inc(x_loaded, 16)

            def load_o(b):
                for h in range(2):
                    sp.dma_start(words(o[h][:]), pr.o[after[0].name][h][bass.ds(b * ko, ko)]
                                 .rearrange("g p n -> p g n")).then_inc(o_loaded, 16)

            def load_context(b):
                for h, src in enumerate((pr.ctx_hi, pr.ctx_lo)):
                    sp.dma_start(words(c[h][:]), src[bass.ds(b, 1)].rearrange("b p t s -> (b p) t s"))\
                        .then_inc(c_loaded, 16)

            def rows_of(scr, b, m, c0, w):
                flat = scr.rearrange("(b g) r s -> b (g r) s", b=B)
                return flat[bass.ds(b, 1), m * P:(m + 1) * P, c0:c0 + w].rearrange("b r s -> (b r) s")

            def store_split(b, n, scr, m, c0, w):
                sp.wait_ge(d_read, 1 + b * ND + at["q"] + n + 1)
                for part, src in zip(scr, (sp_hi, sp_lo)):
                    sp.dma_start(rows_of(part, b, m, c0, w), words(src[:, n % 4, 0:w]))\
                        .then_inc(split_stored[n % 4], 16)

            def element(b, more):
                sp.wait_ge(d_read, 1 + b * ND + (at["ln_attn"] + 1 if attn else x_final))
                if x_out is not None:
                    sp.dma_start(x_out[bass.ds(b, 1)].rearrange("b p t n -> (b p) t n"), x[:])\
                        .then_inc(x_stored, 16)
                if more:
                    if after:
                        load_o(b + 1)
                    if x_out is not None:
                        sp.wait_ge(x_stored, 16 * (b + 1))
                    load_x(b + 1)
                if attn:
                    for m in range(qt):
                        store_split(b, m, pr.q[a.name], m, 0, NQ)
                    for m in range(qt):
                        for n, (c0, w) in enumerate(kcols):
                            store_split(b, qt + m * len(kcols) + n, pr.k[a.name], m, c0, w)
                    for ch in range(NV):
                        sp.wait_ge(a_read, 1 + b * NA + N_GATE + (ch + 1) * vhalf)
                        r = a.chunk_rows(ch)
                        dst = pr.v[a.name][bass.ds(b * a.groups_b, a.groups_b), 0:r, ch, :]
                        sp.dma_start(dst.rearrange("g p m -> p g m"),
                                     v_sb[0:r, ch % 2, :].rearrange("p (g m) -> p g m", m=P))\
                            .then_inc(v_stored[ch % 2], 16)
                    if more and a.cross:
                        load_context(b + 1)

            for stored in split_stored + v_stored:
                sp.sem_inc(stored, 1)
            load_x(0)
            if after:
                load_o(0)
            if attn and a.cross:
                load_context(0)
            for i, piece in enumerate(pieces):
                if i >= 2:
                    sp.wait_ge(w_split, i - 1)
                sp.dma_start(raw_piece(i), piece[0]).then_inc(w_raw[i % 2], 16)
            with sp.Fori(0, B - 1, 1) as b:
                element(b, True)
            element(B - 1, False)
            if x_out is not None:
                sp.wait_ge(x_stored, 16 * B)
            if attn:
                for s in range(4):
                    if uses[s]:
                        sp.wait_ge(split_stored[s], 1 + 32 * B * uses[s])
                for s in range(2):
                    sp.wait_ge(v_stored[s], 1 + 16 * B * v_uses[s])

        @block.gpsimd
        def _(pool):
            pr.clear_old(pool)
            if attn and a.layer == 1:
                pad = v_sb[:].rearrange("p s (h m) -> p (s h) m", m=32)
                nc.gpsimd.memset(pad[:, :, 16:32], 0.0).then_inc(pad_done, 1)
                pool.wait_ge(pad_done, 1)
                nc.gpsimd.memset(pad[:, :, 16:17], 1.0).then_inc(pad_done, 1)

        @block.tensor
        def _(pe):
            pe.wait_ge(w_split, len(pieces))
            with pe.Fori(0, B, 1) as b:
                d = 0
                ac = 0

                def d_bank():
                    pe.wait_ge(d_read, 1 + b * ND + max(d - 3, 0))
                    return ps[:, d % 4, :]

                def a_bank():
                    pe.wait_ge(a_read, 1 + b * NA + max(ac - 3, 0))
                    return ps[:, 4 + ac % 4, :]

                ln = 0

                def mean_and_var():
                    nonlocal d, ln
                    base = (b * n_ln + ln) * LN_DVE
                    for what, src in ((0, x), (1, sq)):
                        if what:
                            pe.wait_ge(ln_act, (b * n_ln + ln) * LN_ACT + 1)
                        out = d_bank()
                        for kt in range(KT):
                            last = nc.tensor.matmul(out, pr.mean_ones[:], src[:, kt, :],
                                                    start=(kt == 0), stop=(kt == KT - 1))
                        last.then_inc(d_tile, 1)
                        d += 1
                    pe.wait_ge(ln_dve, base + LN_DVE)
                    ln += 1

                pe.wait_ge(x_loaded, 16 * (b + 1))
                if after:
                    pe.wait_ge(o_loaded, 32 * (b + 1))
                    for m in range(KT):
                        product3(pe, d_bank(), wo, (slice(m * P, (m + 1) * P),), o, (slice(None),), ko)\
                            .then_inc(d_tile, 1)
                        d += 1
                    pe.wait_ge(d_read, 1 + b * ND + d)
                if ff:
                    mean_and_var()
                    for m in range(FT):
                        g0 = FF * geglu + m * P
                        product3(pe, a_bank(), w1, (slice(g0, g0 + P),), z, (slice(None),), KT)\
                            .then_inc(a_tile, 1)
                        ac += 1
                        if geglu:
                            product3(pe, d_bank(), w1, (slice(m * P, (m + 1) * P),), z, (slice(None),), KT)\
                                .then_inc(d_tile, 1)
                            d += 1
                    pe.wait_ge(u_lo, 1 + (b + 1) * FT)
                    for m in range(KT):
                        product3(pe, d_bank(), w2, (slice(m * P, (m + 1) * P),), u, (slice(None),), FT)\
                            .then_inc(d_tile, 1)
                        d += 1
                    if attn:
                        pe.wait_ge(d_read, 1 + b * ND + d)
                if attn:
                    mean_and_var()
                    for m in range(qt):
                        product3(pe, d_bank(), wq, (slice(m * P, (m + 1) * P),), z, (slice(None),), KT)\
                            .then_inc(d_tile, 1)
                        d += 1
                    src, kts = (c, 2) if a.cross else (z, KT)
                    if a.cross:
                        pe.wait_ge(c_loaded, 32 * (b + 1))
                    for m in range(qt):
                        for c0, w in kcols:
                            product3(pe, d_bank()[:, 0:w], wk, (slice(m * P, (m + 1) * P),), src,
                                     (slice(c0, c0 + w),), kts).then_inc(d_tile, 1)
                            d += 1
                    for ch in range(NV):
                        r = a.chunk_rows(ch)
                        for hf in range(vhalf):
                            product3(pe, a_bank()[0:r, 0:vw], src, (slice(ch * P, ch * P + r),), wv,
                                     (slice(hf * vw, (hf + 1) * vw),), kts).then_inc(a_tile, 1)
                            ac += 1
                assert (d, ac) == (ND, NA)

        @block.scalar
        def _(act):
            for i in range(len(pieces)):
                act.wait_ge(w_raw[i % 2], 16 * (i // 2 + 1))
                nc.scalar.copy(pieces[i][1], raw_piece(i)).then_inc(w_hi, 1)
            act.sem_inc(a_read, 1)
            with act.Fori(0, B, 1) as b:
                d = ac = ln = 0

                def layernorm_act(gain):
                    nonlocal d, ln
                    act.wait_ge(d_read, 1 + b * ND + d + 1)
                    nc.scalar.activation(sq[:], xc[:], ACT.Square).then_inc(ln_act, 1)
                    act.wait_ge(ln_dve, (b * n_ln + ln) * LN_DVE + 1)
                    nc.scalar.activation(dev[:], var[:], ACT.Sqrt).then_inc(ln_act, 1)
                    act.wait_ge(ln_dve, (b * n_ln + ln) * LN_DVE + 2)
                    for kt in range(KT):
                        last = nc.scalar.activation(z[0][:, kt, :], ud[:, kt, :], ACT.Identity,
                                                    bias=pr.vcol(gain[1], kt))
                    last.then_inc(ln_act, 1)
                    d += 2
                    ln += 1

                if after:
                    d += KT
                if ff:
                    layernorm_act(ff[1:3])
                    bias = ff[4]

                    def u_round(m):
                        if geglu:
                            act.wait_ge(d_read, 1 + b * ND + at["ff_a"] + m + 1)
                        else:
                            act.wait_ge(a_read, 1 + b * NA + m + 1)
                        nc.scalar.copy(u[0][:, m, :], uf[:, m % 2, :]).then_inc(u_hi, 1)

                    for m in range(FT):
                        act.wait_ge(a_tile, b * NA + ac + 1)
                        if geglu:
                            act.wait_ge(d_read, 1 + b * ND + at["ff_a"] + max(m - 1, 0))
                        else:
                            act.wait_ge(u_lo, 1 + b * FT + max(m - 1, 0))
                        done = nc.scalar.activation(gate[:, m % 2, :], ps[:, 4 + ac % 4, :], ACT.Gelu,
                                                    bias=pr.vcol(bias, FT * geglu + m))
                        done.then_inc(a_read, 1)
                        ac += 1
                        if geglu:
                            d += 1
                        if m:
                            u_round(m - 1)
                    u_round(FT - 1)
                    d += KT
                if attn:
                    layernorm_act(attn[1:3])
                    for m in range(NSPLIT):
                        w = NQ if m < qt else kcols[(m - qt) % len(kcols)][1]
                        act.wait_ge(d_tile, b * ND + d + 1)
                        act.wait_ge(split_stored[m % 4], 1 + 32 * (b * uses[m % 4] + m // 4))
                        nc.scalar.copy(sp_hi[:, m % 4, 0:w], ps[:, d % 4, 0:w]).then_inc(hi_done, 1)
                        d += 1
                    if a.layer == 1:
                        act.wait_ge(pad_done, 2)
                    for ch in range(NV):
                        r = a.chunk_rows(ch)
                        act.wait_ge(v_stored[ch % 2], 1 + 16 * (b * v_uses[ch % 2] + ch // 2))
                        for hf in range(vhalf):
                            act.wait_ge(a_tile, b * NA + ac + 1)
                            src = ps[0:r, 4 + ac % 4, 0:vw]
                            if a.layer == 0:
                                dst = v_sb[0:r, ch % 2, hf * vw:(hf + 1) * vw]
                            else:
                                dst = v_sb[0:r, ch % 2, :].rearrange("p (h m) -> p h m", m=32)[:, :, 0:16]
                                src = src.rearrange("p (h m) -> p h m", m=16)
                            nc.scalar.copy(dst, src).then_inc(a_read, 1)
                            ac += 1

        @block.vector
        def _(dve):
            for i in range(len(pieces)):
                dve.wait_ge(w_hi, i + 1)
                nc.vector.tensor_tensor(pieces[i][2], raw_piece(i), pieces[i][1].bitcast(F32), ALU.subtract)\
                    .then_inc(w_split, 1)
            dve.sem_inc(d_read, 1)
            dve.sem_inc(u_lo, 1)
            with dve.Fori(0, B, 1) as b:
                d = ln = 0

                def next_tile():
                    dve.wait_ge(d_tile, b * ND + d + 1)
                    return ps[:, d % 4, :]

                def layernorm_dve(gain):
                    nonlocal d, ln
                    dbase, abase = (b * n_ln + ln) * LN_DVE, (b * n_ln + ln) * LN_ACT
                    mean = next_tile()
                    for kt in range(KT):
                        last = nc.vector.tensor_tensor(xc[:, kt, :], x[:, kt, :], mean, ALU.subtract)
                    last.then_inc(d_read, 1)
                    d += 1
                    nc.vector.tensor_scalar(var[:], next_tile(), EPS, None, ALU.add).then_inc(d_read, 1)
                    d += 1
                    dve.wait_ge(d_read, 1 + b * ND + d)
                    nc.vector.reciprocal(var[:], var[:]).then_inc(ln_dve, 1)
                    dve.wait_ge(ln_act, abase + 2)
                    for kt in range(KT):
                        last = nc.vector.scalar_tensor_tensor(
                            out=ud[:, kt, :], in0=xc[:, kt, :], scalar=pr.vcol(gain[0], kt), in1=dev[:],
                            op0=ALU.mult, op1=ALU.mult)
                    last.then_inc(ln_dve, 1)
                    dve.wait_ge(ln_act, abase + 3)
                    for kt in range(KT):
                        last = nc.vector.scalar_tensor_tensor(
                            out=z[1][:, kt, :], in0=ud[:, kt, :], scalar=pr.vcol(gain[1], kt),
                            in1=z[0][:, kt, :].bitcast(F32), op0=ALU.add, op1=ALU.subtract)
                    last.then_inc(ln_dve, 1)
                    ln += 1

                def residual(bias):
                    nonlocal d
                    for m in range(KT):
                        nc.vector.scalar_tensor_tensor(out=x[:, m, :], in0=next_tile(), scalar=pr.vcol(bias, m),
                                                       in1=x[:, m, :], op0=ALU.add, op1=ALU.add)\
                            .then_inc(d_read, 1)
                        d += 1
                    dve.wait_ge(d_read, 1 + b * ND + d)

                dve.wait_ge(x_loaded, 16 * (b + 1))
                if after:
                    residual(after[2])
                if ff:
                    layernorm_dve(ff[1:3])

                    def u_low(m):
                        dve.wait_ge(u_hi, b * FT + m + 1)
                        nc.vector.tensor_tensor(u[1][:, m, :], uf[:, m % 2, :], u[0][:, m, :].bitcast(F32),
                                                ALU.subtract).then_inc(u_lo, 1)

                    for m in range(FT):
                        if geglu:
                            t = next_tile()
                            dve.wait_ge(a_read, 1 + b * NA + m + 1)
                            dve.wait_ge(u_lo, 1 + b * FT + max(m - 1, 0))
                            nc.vector.scalar_tensor_tensor(
                                out=uf[:, m % 2, :], in0=t, scalar=pr.vcol(ff[4], m), in1=gate[:, m % 2, :],
                                op0=ALU.add, op1=ALU.mult).then_inc(d_read, 1)
                            d += 1
                        if m:
                            u_low(m - 1)
                    u_low(FT - 1)
                    residual(ff[6])
                if attn:
                    layernorm_dve(attn[1:3])
                    for m in range(NSPLIT):
                        w = NQ if m < qt else kcols[(m - qt) % len(kcols)][1]
                        t = next_tile()
                        dve.wait_ge(hi_done, b * NSPLIT + m + 1)
                        nc.vector.tensor_tensor(sp_lo[:, m % 4, 0:w], t[:, 0:w],
                                                sp_hi[:, m % 4, 0:w].bitcast(F32), ALU.subtract)\
                            .then_inc(d_read, 1)
                        d += 1


def attend_phase(pr, name, a):
    nc = pr.nc
    pr.start_phase()
    G, M, NC, NCP, U, NG, KP, NB, S = a.G, a.M, a.NC, a.NCP, a.U, a.NG, a.kp, a.NB, a.keys
    wide = a.layer == 0
    SLOTS = 3 if a.cross else 4
    RC = SLOTS
    IH = 4 * NB
    NI = IH * G
    NLOAD = (7 if wide else 9) + (NC * P > S)
    PIECE = P
    E = NC * G
    MXB, SCB = (3, 3) if a.cross else (4, 2)
    assert SLOTS * NI % MXB == 0 and SLOTS * E % SCB == 0

    def chunk_step(cp, h, k):
        return 2 * G * cp + len(a.pair(cp)) * h + k

    def items_until(u):
        return min(NI, -(-(u + 1) * NI // (U - 1)))

    row_at = [min(U - 1, next(u for u in range(U) if items_until(u) >= (h + 1) * IH) + 1) for h in range(G)]
    row_at[G - 1] = U

    def value_at(j):
        return j // 2 * G + G + 1 + j % 2 * (G // 2)

    RAW_AT = value_at(NC - 1) + 1
    MERGE_AT = U + (1 if NCP > 2 else 2)
    DEN_AT = U + 3 if wide else RAW_AT + 1
    DEN_COPY_AT = DEN_AT + 1
    if NCP > 2:
        RECIP_AT = [DEN_AT + 2 + (1 if wide else 2) * k for k in range(4)]
        DIVIDE_AT = RECIP_AT[3] + 1
    elif wide:
        RECIP_AT, DIVIDE_AT = [DEN_AT + 1, DEN_AT + 1, DEN_AT + 2, DEN_AT + 2], DEN_AT + 2
    else:
        RECIP_AT = [DEN_AT + 2 + k for k in range(4)]
        DIVIDE_AT = RECIP_AT[3]
    HIGH_AT = DIVIDE_AT + 1
    LOW_AT = HIGH_AT + 1
    PEEL = 2
    assert LOW_AT < (PEEL + 1) * U
    DEN_BACK, DEN_U = DEN_AT // U, DEN_AT % U
    early_rows = sum(p <= DEN_U for p in row_at)

    pool_sums = [(cp, h) for cp in range(1, min(NCP, 6)) for h in range(G)]
    dve_sums = [(cp, h) for cp in range(6, NCP) for h in range(G)] if wide else []

    def sem(what):
        return pr.sem(f"{name}_{what}")

    loaded = [sem(f"loaded{r}") for r in range(SLOTS)]
    zeros_set, first_zeros, ones_set = sem("zeros_set"), sem("first_zeros"), sem("ones_set")
    item_done, item_read, max_done = sem("item_done"), sem("item_read"), sem("max_done")
    row_done, row_copied = sem("row_done"), sem("row_copied")
    st_done, exp_done, pv_done, pv_copied = sem("st_done"), sem("exp_done"), sem("pv_done"), sem("pv_copied")
    pool_sum, dve_sum, merged = sem("pool_sum"), sem("dve_sum"), sem("merged")
    den_done, den_copied, inverted, divided = sem("den_done"), sem("den_copied"), sem("inverted"), sem("divided")
    o_hi_done, o_lo_done = sem("o_hi_done"), sem("o_lo_done")
    o_stored = [sem(f"o_stored{s}") for s in range(SLOTS)]

    with ExitStack() as st:
        def sb(what, shape, dt=F32):
            return st.enter_context(nc.sbuf_tensor(f"{name}_{what}", shape, dt))

        MR = 64 if wide else 96
        ROWS = 65 if wide else P
        kst = [sb(f"k_stack{r}", [P, G, KP], F32R) for r in range(SLOTS)]
        qst = [sb(f"q_stack{r}", [P, G, NQ], F32R) for r in range(SLOTS)]
        k2 = [sb(f"k_second{r}", [65, G, KP], F32R) for r in range(SLOTS)] if wide else kst
        q2 = [sb(f"q_second{r}", [65, G, NQ], F32R) for r in range(SLOTS)] if wide else qst
        v = [sb(f"v{r}", [P, NC, P]) for r in range(SLOTS)]
        prob = sb("prob", [P, RC, G, 2, BANK])
        blk_max = sb("blk_max", [P, SLOTS, G, 4, NB])
        row_max = sb("row_max", [P, SLOTS, G, 4, 1]) if NB > 1 else blk_max
        if wide:
            prob_sum = sb("prob_sum", [P, G, 2, BANK])
            chunk_sum = sb("chunk_sum", [P, G, NQ])
        den = sb("den", [P, SLOTS, NQ])
        o_full = sb("o_full", [P, SLOTS, NQ])
        o_hi, o_lo = sb("o_hi", [P, SLOTS, NQ], F32R), sb("o_lo", [P, SLOTS, NQ], F32R)
        mx = st.enter_context(nc.psum_tensor(f"{name}_mx", [P, MXB, BANK], F32))
        sc = st.enter_context(nc.psum_tensor(f"{name}_sc", [P, SCB, BANK], F32))
        pv = st.enter_context(nc.psum_tensor(f"{name}_pv", [P, BANK], F32))
        aux = st.enter_context(nc.psum_tensor(f"{name}_aux", [P, BANK], F32))
        block = st.enter_context(nc.Block())

        def prob_of(c, cp, h):
            return prob[:, (c * NCP + cp) % RC, h]

        def groups(eng, body, end):
            for i in range(PEEL):
                body(i // SLOTS, i % SLOTS, i)
            rounds = (NG - PEEL - end) // SLOTS
            with eng.Fori(0, rounds, 1) as q:
                for c in range(PEEL, PEEL + SLOTS):
                    body(q, c, None)
            for i in range(PEEL + SLOTS * rounds, NG):
                body(i // SLOTS, i % SLOTS, i)

        def late(u, at):
            return at // U if at % U == u else 0

        def exists(n, back):
            return n is None or n >= back

        def drain(steps):
            todo = [(g * U + at, g, step) for at, step in steps for g in range(NG - PEEL, NG)
                    if g * U + at >= NG * U]
            for _, g, step in sorted(todo, key=lambda x: x[0]):
                step(g // SLOTS, g % SLOTS)

        @block.sync
        def _(sp):
            def load(q, c):
                r, one = c % SLOTS, bass.ds(SLOTS * q + c, 1)
                k_hi, k_lo = (t[one].rearrange("g (h r) s -> r (g h) s", h=G) for t in pr.k[a.name])
                q_hi, q_lo = (t[one].rearrange("g (h r) s -> r (g h) s", h=G) for t in pr.q[a.name])
                if wide:
                    moves = [(kst[r][0:64], k_hi), (kst[r][64:128], k_lo), (qst[r][0:64], q_hi),
                             (qst[r][64:128], q_hi), (k2[r][0:64], k_hi), (q2[r][0:64], q_lo)]
                else:
                    moves = [(kst[r][16 * n:16 * n + 16], (k_hi, k_lo)[n % 2]) for n in range(4)]
                    moves += [(qst[r][16 * n:16 * n + 16], (q_hi, q_lo)[n // 2]) for n in range(4)]
                vs = pr.v[a.name][one].rearrange("g p c m -> (g p) c m")
                full = S // P
                moves.append((v[r][:, 0:full, :], vs[:, 0:full, :]))
                if full < NC:
                    rows = a.chunk_rows(full)
                    moves.append((v[r][0:rows, full:NC, :], vs[0:rows, full:NC, :]))
                assert len(moves) == NLOAD
                for dst, src in moves:
                    sp.dma_start(words(dst), src).then_inc(loaded[r], 16)

            def store(q, c):
                r, i = c % SLOTS, SLOTS * q + c
                sp.wait_ge(o_lo_done, i + 1)
                for dst, src in zip(pr.o[a.name], (o_hi, o_lo)):
                    sp.dma_start(dst[bass.ds(i, 1)].rearrange("i p n -> (i p) n"), words(src[:, r, :]))\
                        .then_inc(o_stored[r], 16)

            def main(q, c, n):
                if n != 0:
                    sp.wait_ge(pv_done, (SLOTS * q + c) * NC)
                if n is None or n + SLOTS - 1 < NG:
                    load(q, c + SLOTS - 1)
                if exists(n, LOW_AT // U):
                    store(q, c - LOW_AT // U)

            for stored in o_stored:
                sp.sem_inc(stored, 1)
            for g in range(SLOTS - 1):
                load(0, g)
            groups(sp, main, SLOTS - 1)
            for g in range(NG - LOW_AT // U, NG):
                store(g // SLOTS, g % SLOTS)
            for r in range(SLOTS):
                sp.wait_ge(o_stored[r], 1 + 32 * len(range(r, NG, SLOTS)))

        @block.gpsimd
        def _(pool):
            pr.clear_old(pool)
            if not wide:
                for r in range(1, SLOTS):
                    nc.gpsimd.memset(kst[r][64:P].bitcast(F32), 0.0).then_inc(zeros_set, 1)
                    nc.gpsimd.memset(qst[r][64:P].bitcast(F32), 0.0).then_inc(zeros_set, 1)
                pool.wait_ge(zeros_set, 2 * SLOTS)
            for r in range(SLOTS):
                nc.gpsimd.memset(k2[r][MR:MR + 1].bitcast(F32), 1.0).then_inc(ones_set, 1)

            def main(q, c, n):
                i = SLOTS * q + c
                for m, (cp, h) in enumerate(pool_sums):
                    pool.wait_ge(exp_done, i * E + chunk_step(cp, h + 1, 0))
                    if cp == 1:
                        if n != 0:
                            pool.wait_ge(merged, (i - 1) * G + h + 1)
                        other = prob_of(c, 0, h)
                    else:
                        pool.wait_ge(pool_sum, i * len(pool_sums) + m - G + 1)
                        other = prob_sum[:, h]
                    nc.gpsimd.tensor_tensor(prob_sum[:, h], prob_of(c, cp, h), other, ALU.add)\
                        .then_inc(pool_sum, 1)

            if wide:
                groups(pool, main, 1)

        @block.tensor
        def _(pe):
            def item(q, c, n, m):
                r, i = c % SLOTS, SLOTS * q + c
                if m == 0:
                    pe.wait_ge(loaded[r], 16 * NLOAD * (q + c // SLOTS + 1))
                rows = P if wide else 96
                h, t, at = m // IH, m % IH // NB, a.block_at[m % NB]
                if not (n == 0 and m < MXB):
                    pe.wait_ge(item_read, i * NI + m - MXB + 1)
                nc.tensor.matmul(mx[:, (c * NI + m) % MXB, 0:a.blk], qst[r][0:rows, h, t * P:(t + 1) * P],
                                 kst[r][0:rows, h, at:at + a.blk], start=True, stop=True)\
                    .then_inc(item_done, 1)

            def row(q, c, h, n, dens):
                r, i = c % SLOTS, SLOTS * q + c
                if NB > 1:
                    pe.wait_ge(max_done, i * G + h + 1)
                else:
                    pe.wait_ge(item_read, i * NI + (h + 1) * IH)
                if not (n == 0 and h == 0):
                    pe.wait_ge(row_copied, i * G + h)
                if not (isinstance(dens, int) and dens <= 0):
                    pe.wait_ge(den_copied, dens)
                for t in range(4):
                    last = nc.tensor.transpose(aux[0:1, t * P:(t + 1) * P], row_max[:, r, h, t], pr.ident[:])
                last.then_inc(row_done, 1)

            def scores(q, c, u, k, n):
                r, cp, h = c % SLOTS, u // G, u % G
                ch, e = 2 * cp + k, chunk_step(cp, h, k)
                rows, k0 = a.chunk_rows(ch), ch * P
                if not (n == 0 and e < SCB):
                    pe.wait_ge(exp_done, (SLOTS * q + c) * E + e - SCB + 1)
                out = sc[0:rows, (c * E + e) % SCB, :]
                if wide:
                    nc.tensor.matmul(out, kst[r][:, h, k0:k0 + rows], qst[r][:, h, :], start=True, stop=False)
                nc.tensor.matmul(out, k2[r][0:ROWS, h, k0:k0 + rows], q2[r][0:ROWS, h, :],
                                 start=not wide, stop=True).then_inc(st_done, 1)

            def values(q, c, j):
                r, i, cp = c % SLOTS, SLOTS * q + c, j // 2
                pe.wait_ge(exp_done, i * E + min(NC, 2 * cp + 2) * G)
                if j == 0 and not (isinstance(i, int) and i == 0):
                    pe.wait_ge(pv_copied, i)
                rows = a.chunk_rows(j)
                for h in range(G):
                    last = nc.tensor.matmul(pv[h * M:(h + 1) * M, :], v[r][0:rows, j, h * M:(h + 1) * M],
                                            prob_of(c, cp, h)[0:rows, j % 2, :],
                                            start=(j == 0), stop=(j == NC - 1))
                last.then_inc(pv_done, 1)

            def denominators(q, c, rows_before):
                r, i = c % SLOTS, SLOTS * q + c
                pe.wait_ge(row_copied, rows_before)
                if DEN_BACK > 1 or not isinstance(i, int) or i:
                    if not (isinstance(i, int) and i == 0):
                        pe.wait_ge(den_copied, i)
                if wide:
                    pe.wait_ge(merged, (i + 1) * G)
                    for h in range(G):
                        last = nc.tensor.matmul(aux[h * M:(h + 1) * M, :], pr.ones[:, 0:M],
                                                chunk_sum[:, h, :], start=True, stop=True)
                else:
                    pe.wait_ge(pv_copied, i + 1)
                    last = nc.tensor.matmul(aux[:], pr.den_sel[:], o_full[:, r, :], start=True, stop=True)
                last.then_inc(den_done, 1)

            def main(q, c, n):
                i, ahead, done = SLOTS * q + c, n != NG - 1, 0
                for u in range(U):
                    todo = list(range(done, items_until(u))) if ahead else []
                    done = items_until(u)

                    def next_item():
                        if todo:
                            item(q, c + 1, None, todo.pop(0))

                    if u < G:
                        pe.wait_ge(row_copied, i * G + u + 1)
                    for k in range(len(a.pair(u // G))):
                        scores(q, c, u, k, n)
                        next_item()
                    if u == 0:
                        row(q, c, G - 1, n, i - DEN_BACK)
                    if ahead:
                        for h in range(G):
                            if row_at[h] == u:
                                row(q, c + 1, h, None, i - DEN_BACK + (DEN_U < u))
                    for j in range(NC):
                        back = value_at(j) // U
                        if value_at(j) % U == u and exists(n, back):
                            values(q, c - back, j)
                            next_item()
                    while todo:
                        next_item()
                    if DEN_U == u and exists(n, DEN_BACK):
                        denominators(q, c - DEN_BACK, (i + 1) * G + (early_rows if ahead else 0))

            if not wide:
                pe.wait_ge(first_zeros, 2)
            for m in range(NI):
                item(0, 0, 0, m)
            pe.wait_ge(ones_set, SLOTS)
            for h in range(G - 1):
                row(0, 0, h, 0, 0)
            groups(pe, main, 1)
            drain([(value_at(j), lambda q, c, j=j: values(q, c, j)) for j in range(NC)]
                  + [(DEN_AT, lambda q, c: denominators(q, c, NG * G))])

        @block.scalar
        def _(act):
            def row_copy(q, c, h):
                r, i = c % SLOTS, SLOTS * q + c
                act.wait_ge(row_done, i * G + h + 1)
                nc.scalar.activation(q2[r][MR:MR + 1, h, :], aux[0:1, :], ACT.Copy, scale=-1.0)\
                    .then_inc(row_copied, 1)

            def exps(q, c, u, known):
                i, cp, h = SLOTS * q + c, u // G, u % G
                back, cpb = -((cp - RC) // NCP), (cp - RC) % NCP
                if exists(known, back):
                    act.wait_ge(pv_done, (i - back) * NC + min(NC, 2 * cpb + 2))
                    if wide:
                        unit = (max(cpb, 1), h)
                        if unit in pool_sums:
                            act.wait_ge(pool_sum, (i - back) * len(pool_sums) + pool_sums.index(unit) + 1)
                        else:
                            act.wait_ge(dve_sum, (i - back) * len(dve_sums) + dve_sums.index(unit) + 1)
                for k, ch in enumerate(a.pair(cp)):
                    rows, e = a.chunk_rows(ch), chunk_step(cp, h, k)
                    act.wait_ge(st_done, i * E + e + 1)
                    nc.scalar.activation(prob_of(c, cp, h)[0:rows, k, :], sc[0:rows, (c * E + e) % SCB, :],
                                         ACT.Exp, scale=a.scale).then_inc(exp_done, 1)

            def raw_copy(q, c):
                i = SLOTS * q + c
                act.wait_ge(pv_done, (i + 1) * NC)
                nc.scalar.copy(o_full[:, c % SLOTS, :], pv[:]).then_inc(pv_copied, 1)

            def den_copy(q, c):
                i = SLOTS * q + c
                act.wait_ge(den_done, i + 1)
                nc.scalar.copy(den[:, c % SLOTS, :], aux[:]).then_inc(den_copied, 1)

            def high_part(q, c):
                i = SLOTS * q + c
                act.wait_ge(divided, i + 1)
                if not (isinstance(i, int) and i < SLOTS):
                    act.wait_ge(o_stored[c % SLOTS], 1 + 32 * (q + c // SLOTS))
                nc.scalar.copy(o_hi[:, c % SLOTS, :], o_full[:, c % SLOTS, :]).then_inc(o_hi_done, 1)

            steps = [(RAW_AT, raw_copy), (DEN_COPY_AT, den_copy), (HIGH_AT, high_part)]

            def main(q, c, n):
                for u in range(U):
                    for at, step in steps:
                        if late(u, at) and exists(n, late(u, at)):
                            step(q, c - late(u, at))
                    exps(q, c, u, n)
                    if u == 0:
                        row_copy(q, c, G - 1)
                    if n != NG - 1:
                        for h in range(G):
                            if row_at[h] == u:
                                row_copy(q, c + 1, h)

            for h in range(G - 1):
                row_copy(0, 0, h)
            groups(act, main, 1)
            drain(steps)

        @block.vector
        def _(dve):
            def items(q, c, done, until):
                r, i = c % SLOTS, SLOTS * q + c
                for n in range(done, until):
                    h, t, nb = n // IH, n % IH // NB, n % NB
                    dve.wait_ge(item_done, i * NI + n + 1)
                    nc.vector.reduce_max(blk_max[:, r, h, t, nb:nb + 1], mx[:, (c * NI + n) % MXB, 0:a.blk], AX.X)\
                        .then_inc(item_read, 1)
                    if NB > 1 and n % IH == IH - 1:
                        dve.wait_ge(item_read, i * NI + n + 1)
                        nc.vector.reduce_max(row_max[:, r, h, :, 0], blk_max[:, r, h], AX.X)\
                            .then_inc(max_done, 1)

            def last_sums(q, c):
                i = SLOTS * q + c
                for n, (cp, h) in enumerate(dve_sums):
                    rows = a.chunk_rows(2 * cp)
                    dve.wait_ge(exp_done, i * E + chunk_step(cp, h + 1, 0))
                    dve.wait_ge(pool_sum, i * len(pool_sums) + len(pool_sums) - G + h + 1)
                    nc.vector.tensor_tensor(prob_sum[0:rows, h, 0, :], prob_sum[0:rows, h, 0, :],
                                            prob_of(c, cp, h)[0:rows, 0, :], ALU.add).then_inc(dve_sum, 1)

            def merge(q, c):
                i = SLOTS * q + c
                if not (isinstance(i, int) and i == 0):
                    dve.wait_ge(den_done, i)
                for h in range(G):
                    dve.wait_ge(pool_sum, i * len(pool_sums) + len(pool_sums) - G + h + 1)
                    if dve_sums:
                        dve.wait_ge(dve_sum, i * len(dve_sums) + h + 1)
                    nc.vector.tensor_tensor(chunk_sum[:, h, :], prob_sum[:, h, 0, :], prob_sum[:, h, 1, :],
                                            ALU.add).then_inc(merged, 1)

            def invert(q, c, k):
                dve.wait_ge(den_copied, SLOTS * q + c + 1)
                piece = den[:, c % SLOTS, k * PIECE:(k + 1) * PIECE]
                nc.vector.reciprocal(piece, piece).then_inc(inverted, 1)

            def divide(q, c):
                i = SLOTS * q + c
                dve.wait_ge(inverted, 4 * (i + 1))
                dve.wait_ge(pv_copied, i + 1)
                nc.vector.tensor_tensor(o_full[:, c % SLOTS, :], o_full[:, c % SLOTS, :], den[:, c % SLOTS, :], ALU.mult)\
                    .then_inc(divided, 1)

            def low_part(q, c):
                i = SLOTS * q + c
                dve.wait_ge(o_hi_done, i + 1)
                if not (isinstance(i, int) and i < SLOTS):
                    dve.wait_ge(o_stored[c % SLOTS], 1 + 32 * (q + c // SLOTS))
                nc.vector.tensor_tensor(o_lo[:, c % SLOTS, :], o_full[:, c % SLOTS, :],
                                        o_hi[:, c % SLOTS, :].bitcast(F32), ALU.subtract).then_inc(o_lo_done, 1)

            steps = [(U, last_sums)] * bool(dve_sums) + [(MERGE_AT, merge)] * wide
            steps += [(at, lambda q, c, k=k: invert(q, c, k)) for k, at in enumerate(RECIP_AT)]
            steps += [(DIVIDE_AT, divide), (LOW_AT, low_part)]

            def main(q, c, n):
                done = 0
                for u in range(U):
                    extra = [(step, late(u, at)) for at, step in steps if late(u, at) and exists(n, late(u, at))]
                    until = items_until(u)
                    while extra or (done < until and n != NG - 1):
                        if done < until and n != NG - 1:
                            items(q, c + 1, done, done + 1)
                            done += 1
                        if extra:
                            step, back = extra.pop(0)
                            step(q, c - back)

            if not wide:
                for t in (kst[0], qst[0]):
                    nc.vector.memset(t[64:P].bitcast(F32), 0.0).then_inc(first_zeros, 1)
                dve.wait_ge(first_zeros, 2)
                dve.sem_inc(zeros_set, 2)
            items(0, 0, 0, NI)
            groups(dve, main, 1)
            drain(steps)


def build(nc, ins, out):
    with ExitStack() as keep:
        pr = Program(nc, ins, out, keep)
        w0, w1 = "L0_xattn_", "L1_xattn_"
        setup_phase(pr)
        project_phase(pr, "p0", x_in=ins["x"],
                      attn=(SELF0, w0 + "g1", w0 + "b1", w0 + "Wq1", w0 + "Wk1", w0 + "Wv1"))
        attend_phase(pr, "a0", SELF0)
        project_phase(pr, "p1", x_in=ins["x"], x_out=pr.x, after=(SELF0, w0 + "Wo1", w0 + "bo1"),
                      attn=(CROSS0, w0 + "g2", w0 + "b2", w0 + "Wq2", w0 + "Wk2", w0 + "Wv2"))
        attend_phase(pr, "a1", CROSS0)
        project_phase(pr, "p2", x_in=pr.x, x_out=pr.x, after=(CROSS0, w0 + "Wo2", w0 + "bo2"),
                      ff=("geglu", w0 + "g3", w0 + "b3", w0 + "Wp", w0 + "bp", w0 + "Wf", w0 + "bf"),
                      attn=(SELF1, w1 + "n1_g", w1 + "n1_b", w1 + "sq_w", w1 + "sk_w", w1 + "sv_w"))
        attend_phase(pr, "a2", SELF1)
        project_phase(pr, "p3", x_in=pr.x, x_out=pr.x, after=(SELF1, w1 + "so_w", w1 + "so_b"),
                      ff=("gelu", w1 + "n2_g", w1 + "n2_b", w1 + "f1_w1", w1 + "f1_b1", w1 + "f1_w2", w1 + "f1_b2"),
                      attn=(CROSS1, w1 + "n3_g", w1 + "n3_b", w1 + "cq_w", w1 + "ck_w", w1 + "cv_w"))
        attend_phase(pr, "a3", CROSS1)
        project_phase(pr, "p4", x_in=pr.x, x_out=out, after=(CROSS1, w1 + "co_w", w1 + "co_b"),
                      ff=("gelu", w1 + "n4_g", w1 + "n4_b", w1 + "f2_w1", w1 + "f2_b1", w1 + "f2_w2", w1 + "f2_b2"))


_WEIGHTS = (["L0_xattn_" + w for w in ("Wq1", "Wk1", "Wv1", "Wo1", "Wq2", "Wk2", "Wv2", "Wo2", "Wp", "Wf")]
            + ["L1_xattn_" + w for w in ("sq_w", "sk_w", "sv_w", "so_w", "cq_w", "ck_w", "cv_w", "co_w",
                                         "f1_w1", "f1_w2", "f2_w1", "f2_w2")])


def kernel(**inputs):
    import numpy as _np
    import concourse.bacc as _bacc
    from concourse import mybir as _mybir
    from concourse.bass_utils import run_bass_kernel_spmd as _run

    arr = {k: _np.asarray(v) for k, v in inputs.items()}

    def feature_major(t, p):
        return _np.ascontiguousarray(t.reshape(B, t.shape[1], -1, p).transpose(0, 3, 2, 1))

    arrays = {"x": feature_major(arr["x"], P)}
    ctx = _np.zeros((B, SCP, CTX), arr["ctx_768"].dtype)
    ctx[:, :SC] = arr["ctx_768"]
    arrays["ctx"] = feature_major(ctx, CP)
    arrays["vec"] = _np.ascontiguousarray(
        _np.concatenate([arr[n].reshape(w, P) for n, w in VECTORS]).T)
    for n in _WEIGHTS:
        w = arr[n]
        if n in ("L1_xattn_so_w", "L1_xattn_co_w"):
            wide = _np.zeros((HEADS, 32, DIM), w.dtype)
            wide[:, :16] = w.reshape(HEADS, 16, DIM)
            w = wide.reshape(HEADS * 32, DIM)
        arrays[n] = _np.ascontiguousarray(w)

    nc = _bacc.Bacc("TRN2", target_bir_lowering=False, num_devices=1)
    ins = {n: nc.dram_tensor(n + "_in", t.shape, _mybir.dt.from_np(t.dtype), kind="ExternalInput").ap()
           for n, t in arrays.items()}
    out = nc.dram_tensor("out_x", (B, P, KT, NQ), F32, kind="ExternalOutput").ap()
    build(nc, ins, out)
    r = _run(nc, [{n + "_in": t for n, t in arrays.items()}], core_ids=[0])
    got = r.results[0]["out_x"]
    return _np.ascontiguousarray(got.transpose(0, 3, 2, 1).reshape(B, NQ, DIM))
```

```python
from contextlib import ExitStack

import concourse.bass as bass
from concourse import mybir

F32 = mybir.dt.float32
F32R = mybir.dt.float32r
ALU = mybir.AluOpType
ACT = mybir.ActivationFunctionType
AX = mybir.AxisListType

P = 128
B = 4
NQ = 512
DIM = 256
KT = DIM // P
CTX = 192
CROWS = 2 * P
CREST = CTX - P
SC = 1601
SCP = SC + 1
HEADS = 16
FF = 1024
FT = FF // P
EPS = 1e-5
BANK = 512


class Attention:

    def __init__(self, name, layer, keys, cross):
        self.name, self.layer, self.keys, self.cross = name, layer, keys, cross
        self.dh = 64 if layer == 0 else 16
        self.G = 2 if layer == 0 else 4
        self.M = P // self.G
        self.inner = HEADS * self.dh
        self.groups_b = HEADS // self.G
        self.NG = B * self.groups_b
        self.kp = keys + keys % 2
        self.NC = -(-keys // P)
        self.NCP = -(-self.NC // 2)
        self.U = self.NCP * self.G
        self.scale = self.dh ** -0.5
        self.NB = -(-keys // BANK)
        self.blk = keys if self.NB == 1 else 402
        self.block_at = [0] if self.NB == 1 else [0, 400, 800, keys - 402]
        self.rows = self.inner // self.groups_b

    def chunk_rows(self, c):
        return min(P, self.keys - c * P)

    def pair(self, cp):
        return [c for c in (2 * cp, 2 * cp + 1) if c < self.NC]


SELF0 = Attention("self0", 0, NQ, False)
CROSS0 = Attention("cross0", 0, SC, True)
SELF1 = Attention("self1", 1, NQ, False)
CROSS1 = Attention("cross1", 1, SC, True)

VECTORS = [("L0_xattn_bo1", 2), ("L0_xattn_bo2", 2), ("L0_xattn_bp", 16), ("L0_xattn_bf", 2),
           ("L0_xattn_g1", 2), ("L0_xattn_b1", 2), ("L0_xattn_g2", 2), ("L0_xattn_b2", 2),
           ("L0_xattn_g3", 2), ("L0_xattn_b3", 2), ("L1_xattn_so_b", 2), ("L1_xattn_co_b", 2),
           ("L1_xattn_n1_g", 2), ("L1_xattn_n1_b", 2), ("L1_xattn_n2_g", 2), ("L1_xattn_n2_b", 2),
           ("L1_xattn_n3_g", 2), ("L1_xattn_n3_b", 2), ("L1_xattn_n4_g", 2), ("L1_xattn_n4_b", 2),
           ("L1_xattn_f1_b1", 8), ("L1_xattn_f1_b2", 2), ("L1_xattn_f2_b1", 8), ("L1_xattn_f2_b2", 2)]
VEC_AT, _n = {}, 0
for _name, _w in VECTORS:
    VEC_AT[_name] = _n
    _n += _w
NVEC = _n


def words(ap):
    return ap.bitcast(F32) if ap.dtype == F32R else ap


class Program:

    def __init__(self, nc, ins, out, keep):
        self.nc, self.ins, self.out, self.keep = nc, ins, out, keep
        self.phase_sems, self.old_sems, self.handles, self.old_handles = ExitStack(), ExitStack(), [], []

        def dram(name, shape, dt):
            return nc.dram_tensor(name, shape, dt, kind="Internal").ap()

        self.x = dram("x_scratch", [B, P, KT, NQ], F32)
        self.q, self.k, self.v, self.o = {}, {}, {}, {}
        for a in (SELF0, CROSS0, SELF1, CROSS1):
            self.q[a.name] = [dram(f"q_{p}_{a.name}", [a.NG, a.rows, NQ], F32) for p in ("hi", "lo")]
            self.k[a.name] = [dram(f"k_{p}_{a.name}", [a.NG, a.rows, a.kp], F32) for p in ("hi", "lo")]
            self.v[a.name] = dram(f"v_{a.name}", [a.NG, P, a.NC, P], F32)
            self.o[a.name] = [dram(f"o_{p}_{a.name}", [a.NG, P, NQ], F32) for p in ("hi", "lo")]
        self.vec = self.sbuf("vectors", [P, NVEC], F32)
        self.ones = self.sbuf("ones", [P, P], F32)
        self.mean_ones = self.sbuf("mean_ones", [P, P], F32)
        self.ident = self.sbuf("ident", [P, P], F32)
        self.den_pick = self.sbuf("den_pick", [P, 4], F32)

    def sbuf(self, name, shape, dt):
        return self.keep.enter_context(self.nc.sbuf_tensor(name, shape, dt))

    def sem(self, name):
        handle = self.phase_sems.enter_context(self.nc.semaphore(name))
        self.handles.append(handle)
        return handle

    def start_phase(self):
        self.old_sems.close()
        self.old_sems, self.old_handles = self.phase_sems, self.handles
        self.phase_sems, self.handles = ExitStack(), []

    def clear_old(self, pool):
        for handle in self.old_handles:
            pool.sem_clear(handle)

    def vcol(self, name, t):
        at = VEC_AT[name] + t
        return self.vec[:, at:at + 1]


def setup_phase(pr):
    nc = pr.nc
    pr.start_phase()
    vec_loaded, const_step = pr.sem("vec_loaded"), pr.sem("const_step")
    with ExitStack() as st:
        block = st.enter_context(nc.Block())

        @block.sync
        def _(sp):
            sp.dma_start(pr.vec[:], pr.ins["vec"]).then_inc(vec_loaded, 16)
            sp.wait_ge(vec_loaded, 16)

        @block.gpsimd
        def _(pool):
            nc.gpsimd.memset(pr.ones[:], 1.0)
            nc.gpsimd.memset(pr.mean_ones[:], 1.0 / DIM)
            nc.gpsimd.memset(pr.ident[:], 0.0).then_inc(const_step, 1)
            nc.gpsimd.memset(pr.den_pick[:], 0.0).then_inc(const_step, 1)
            pool.wait_ge(const_step, 2)
            nc.gpsimd.affine_select(out=pr.ident[:], in_=pr.ident[:], compare_op=ALU.not_equal, fill=1.0,
                                    base=0, pattern=[[-1, P]], channel_multiplier=1).then_inc(const_step, 1)
            nc.gpsimd.affine_select(out=pr.den_pick[:], in_=pr.den_pick[:], compare_op=ALU.not_equal, fill=1.0,
                                    base=-16, pattern=[[-32, 4]], channel_multiplier=1).then_inc(const_step, 1)
            pool.wait_ge(const_step, 4)


def project_phase(pr, name, after=None, ff=None, attn=None, x_in=None, x_out=None):
    nc = pr.nc
    pr.start_phase()
    n_ln = (ff is not None) + (attn is not None)
    geglu = ff is not None and ff[0] == "geglu"
    a = attn[0] if attn else None
    cross = a is not None and a.cross
    qt = a.inner // P if attn else 0
    kcols = ([(0, NQ)] if not cross else [(0, 402), (402, 400), (802, 400), (1202, 400)]) if attn else []
    vhalf = a.inner // min(a.inner, BANK) if attn else 0
    vw = a.inner // vhalf if attn else 0
    NV = a.NC if attn else 0

    AHEAD = {("mean", 0), ("var", 0), ("scale", 0), ("shift", 0), ("after", 0), ("after", 1), ("residual", 0)}
    prologue = [("after", 0), ("after", 1), ("residual", 0)] * bool(after)
    prologue += [("mean", 0), ("var", 0), ("scale", 0), ("shift", 0)]
    qs = [("q", m) for m in range(qt)]
    ks = [("k", m) for m in range(qt * len(kcols))]
    vs = [("v", ch) for ch in range(NV)]
    kvs = sorted(ks + vs, key=lambda step: (step[1] + 0.5) / len(ks if step[0] == "k" else vs))
    gates = [("gate", m) for m in range(FT)] + [("gate_end", 0)]
    outs = [("out", m) for m in range(KT)]
    if ff and attn and cross:
        order = (gates[:1] + [("context", 0)] + gates[1:] + outs + [("after", 0), ("mean", 1), ("swap_x", 0)]
                 + ks[:2] + [("var", 1), ("after", 1)] + ks[2:4] + [("scale", 1)] + ks[4:6] + [("shift", 1)]
                 + ks[6:] + [("residual", 0)] + qs + [("mean", 0)] + vs[:3] + [("var", 0)] + vs[3:6]
                 + [("scale", 0)] + vs[6:8] + [("shift", 0)] + vs[8:])
    elif ff and attn:
        order = (gates + outs + [("after", 0), ("mean", 1), ("swap_x", 0), ("var", 1), ("after", 1),
                                 ("scale", 1), ("shift", 1), ("residual", 0)] + qs[:1] + [("mean", 0)] + qs[1:]
                 + ks[:1] + [("var", 0)] + ks[1:] + vs[:2] + [("scale", 0), ("shift", 0)] + vs[2:])
    elif attn and cross:
        order = ([("swap_x", 0)] + qs[:4] + [("context", 0)] + qs[4:] + [("after", 0), ("after", 1),
                 ("residual", 0)] + kvs[:2] + [("mean", 0)] + kvs[2:5] + [("var", 0)] + kvs[5:8] + [("scale", 0)]
                 + kvs[8:10] + [("shift", 0)] + kvs[10:])
    elif attn:
        order = ([("swap_x", 0)] + qs[:4] + [("mean", 0)] + qs[4:6] + [("var", 0)] + qs[6:] + kvs[:5]
                 + [("scale", 0)] + kvs[5:] + [("shift", 0)])
    else:
        order = gates + [("after", 0)] + outs + [("swap_x", 0), ("after", 1), ("residual", 0), ("mean", 0),
                                                 ("var", 0), ("scale", 0), ("shift", 0)]
    last_order = [s for s in order if s not in AHEAD]

    def d_tiles(kind):
        return {"mean": 1, "var": 1, "q": 1, "k": 1, "out": 1, "gate": int(geglu)}.get(kind, 0)

    def a_tiles(kind):
        return {"gate": 1, "v": vhalf}.get(kind, 0)

    PRE = 2
    ND, NA = sum(d_tiles(k) for k, _ in order), sum(a_tiles(k) for k, _ in order)
    GR = 2 if geglu else 3
    NAB = 2 if after else 4
    NSPLIT = qt * (1 + len(kcols))
    SPL = 4
    VPL = 4 if cross and ff else 2
    uses = [len(range(s, NSPLIT, SPL)) for s in range(SPL)]
    v_uses = [len(range(s, NV, VPL)) for s in range(VPL)]
    split_no = {step: n for n, step in enumerate(s for s in order if s[0] in "qk")}

    def ln_no(ln, b):
        return b * n_ln + ln

    def last_ln():
        return n_ln - 1

    def sem(what):
        return pr.sem(f"{name}_{what}")

    w_raw = [sem(f"w_raw{s}") for s in range(5 + bool(ff) + geglu)]
    w_hi, w_split = sem("w_hi"), sem("w_split")
    x_loaded, o_loaded, x_stored = sem("x_loaded"), sem("o_loaded"), sem("x_stored")
    ctx_loaded, ctx_hi_done, ctx_split = sem("ctx_loaded"), sem("ctx_hi_done"), sem("ctx_split")
    d_tile, d_read, a_tile, a_read = sem("d_tile"), sem("d_read"), sem("a_tile"), sem("a_read")
    r_tile, r_read = sem("r_tile"), sem("r_read")
    HALVES = [slice(0, NQ // 2), slice(NQ // 2, NQ)]
    centred = sem("centred")
    squared, inverted, rooted, scaled = sem("squared"), sem("inverted"), sem("rooted"), sem("scaled")
    z_hi_done, z_done = sem("z_hi_done"), sem("z_done")
    u_hi, u_lo, hi_done = sem("u_hi"), sem("u_lo"), sem("hi_done")
    split_stored = [sem(f"split_stored{s}") for s in range(SPL)]
    pad_done = sem("pad_done")
    v_stored = [sem(f"v_stored{s}") for s in range(VPL)]

    with ExitStack() as st:
        def sb(what, shape, dt=F32):
            return st.enter_context(nc.sbuf_tensor(f"{name}_{what}", shape, dt))

        weights = []

        def weight(which, p, t, n):
            pair = [sb(f"{which}_{h}", [p, t, n], F32R) for h in ("hi", "lo")]
            weights.append((which, pair[0], pair[1], p, t, n))
            return pair

        if after:
            ko = after[0].groups_b
            wo = weight(after[1], P, ko, DIM)
        if ff:
            w1 = weight(ff[3], P, KT, FF * (1 + geglu))
            w2 = weight(ff[5], P, FT, DIM)
        if attn:
            wq = weight(attn[3], P, KT, a.inner)
            wk = weight(attn[4], P, KT, a.inner)
            wv = weight(attn[5], P, KT, a.inner)

        x = sb("x", [P, KT, NQ])
        x_from = sb("x_from", [P, KT, NQ]) if after else x
        xc, sq = sb("xc", [P, KT, NQ]), sb("sq", [P, KT, NQ])
        ud = sq if ff and attn else sb("ud", [P, KT, NQ])
        var, dev = sb("var", [P, NQ]), sb("dev", [P, NQ])
        z = [[sb(f"z{ln}_{h}", [P, KT, NQ], F32R) for h in ("hi", "lo")] for ln in range(n_ln)]
        ln_vectors = [x_[1:3] for x_ in (ff, attn) if x_]
        if after:
            o = [sb(f"o_{h}", [P, ko, NQ], F32R) for h in ("hi", "lo")]
        if ff:
            u = [sb(f"u_{h}", [P, FT, NQ], F32R) for h in ("hi", "lo")]
            gate = sb("gate", [P, GR, NQ])
            uf = sb("uf", [P, 2, NQ]) if geglu else gate
        if attn:
            sp_hi, sp_lo = sb("split_hi", [P, SPL, NQ], F32R), sb("split_lo", [P, SPL, NQ], F32R)
            v_sb = sb("v_sb", [P, VPL, a.groups_b * P])
            if cross:
                ctx_raw = sb("ctx_raw", [P, 2, SCP])
                c = [sb(f"c_{h}", [P, 2, SCP], F32R) for h in ("hi", "lo")]
        ps = st.enter_context(nc.psum_tensor(f"{name}_ps", [P, 8, BANK], F32))

        pieces, split_by = [], {}
        for which, hi, lo, p, t, n in weights:
            src = pr.ins[which].rearrange("(t p) n -> p t n", p=p)
            for_context = cross and which in attn[4:6]
            step = 1 if for_context else max(1, 1024 // n)
            for t0 in range(0, t, step):
                for n0 in range(0, n, 1024):
                    n1 = min(n, n0 + 1024)
                    t1 = min(t, t0 + step)
                    stacked = for_context and t0 == 1
                    pieces.append((src[:, t0:t1, n0:n1], hi[:, t0:t1, n0:n1], lo[:, t0:t1, n0:n1],
                                   p, t1 - t0, n1 - n0, stacked))
            split_by[which] = len(pieces)
        rooms = [t[:, 0:2].rearrange("p k n -> p (k n)")
                 for t in [xc, sq] + ([] if ff and attn else [ud]) + ([gate] if ff else [])
                 + ([uf] if geglu else [])]
        if not (ff and attn):
            wtmp = sb("w_tmp", [P, 2, 1024])
            rooms += [wtmp[:, 0, :], wtmp[:, 1, :]]
        NR = len(rooms)

        def raw_piece(i):
            p, t, n = pieces[i][3:6]
            return rooms[i % NR][0:p, 0:t * n].rearrange("p (t n) -> p t n", t=t)

        block = st.enter_context(nc.Block())

        def product3(out, w, wsl, y, ysl, kts):
            n = 0
            for kt in range(kts):
                for wi, yi in ((0, 0), (0, 1), (1, 0)):
                    last = nc.tensor.matmul(out, w[wi][(slice(None), kt) + wsl], y[yi][(slice(None), kt) + ysl],
                                            start=(n == 0), stop=(n == 3 * kts - 1))
                    n += 1
            return last

        def product5(out, x_, xsl, y, ysl):
            pairs = [(x_[0][:, 0], y[0][:, 0]), (x_[0][:, 0], y[1][:, 0]), (x_[1][:, 0], y[0][:, 0]),
                     (x_[0][:, 1], y[0][:, 1])]
            rest = (x_[0], y[1]) if x_ is not c else (x_[1], y[0])
            pairs.append(tuple(t[0:CREST, 1] for t in rest))
            for n, (p_, r_) in enumerate(pairs):
                last = nc.tensor.matmul(out, p_[:, xsl], r_[:, ysl], start=(n == 0), stop=(n == 4))
            return last

        def d_count(b, d):
            return PRE + b * ND + d if b is not None else d

        def k_place(m):
            c0, w = kcols[m % len(kcols)]
            return m // len(kcols), c0, w

        @block.sync
        def _(sp):
            def load_x(b):
                sp.dma_start(x_from[:], x_in[bass.ds(b, 1)].rearrange("b p t n -> (b p) t n")).then_inc(x_loaded, 16)

            def load_o(b):
                for h in range(2):
                    sp.dma_start(words(o[h][:]), pr.o[after[0].name][h][bass.ds(b * ko, ko)]
                                 .rearrange("g p n -> p g n")).then_inc(o_loaded, 16)

            def load_context(b):
                sp.dma_start(ctx_raw[:], pr.ins["ctx"][bass.ds(b, 1)].rearrange("b p t s -> (b p) t s"))\
                    .then_inc(ctx_loaded, 16)

            def rows_of(scr, b, m, c0, w):
                flat = scr.rearrange("(b g) r s -> b (g r) s", b=B)
                return flat[bass.ds(b, 1), m * P:(m + 1) * P, c0:c0 + w].rearrange("b r s -> (b r) s")

            def store_split(b, step, d, scr, m, c0, w):
                n = split_no[step]
                sp.wait_ge(d_read, 1 + d_count(b, d) + 1)
                for part, src in zip(scr, (sp_hi, sp_lo)):
                    sp.dma_start(rows_of(part, b, m, c0, w), words(src[:, n % SPL, 0:w]))\
                        .then_inc(split_stored[n % SPL], 16)

            def element(b, steps, more):
                d = ac = 0
                if after and more:
                    sp.wait_ge(r_read, KT * (b + 1))
                    load_x(b + 1)
                for kind, m in steps:
                    if kind == "swap_x":
                        if x_out is not None:
                            sp.wait_ge(d_read, 1 + d_count(b, d))
                            sp.dma_start(x_out[bass.ds(b, 1)].rearrange("b p t n -> (b p) t n"), x[:])\
                                .then_inc(x_stored, 16)
                        elif more:
                            sp.wait_ge(d_read, 1 + d_count(b, d))
                            load_x(b + 1)
                    elif (kind, m) == ("after", 1) and more > 1:
                        sp.wait_ge(r_tile, KT * (b + 2))
                        load_o(b + 2)
                    elif kind == "context":
                        if more:
                            sp.wait_ge(ctx_split, b + 1)
                            load_context(b + 1)
                    elif kind == "q":
                        store_split(b, (kind, m), d, pr.q[a.name], m, 0, NQ)
                    elif kind == "k":
                        store_split(b, (kind, m), d, pr.k[a.name], *k_place(m))
                    elif kind == "v":
                        sp.wait_ge(a_read, 1 + b * NA + ac + vhalf)
                        r = a.chunk_rows(m)
                        dst = pr.v[a.name][bass.ds(b * a.groups_b, a.groups_b), 0:r, m, :]
                        sp.dma_start(dst.rearrange("g p m -> p g m"),
                                     v_sb[0:r, m % VPL, :].rearrange("p (g m) -> p g m", m=P))\
                            .then_inc(v_stored[m % VPL], 16)
                    d += d_tiles(kind)
                    ac += a_tiles(kind)

            for stored in split_stored + v_stored:
                sp.sem_inc(stored, 1)
            load_x(0)
            for i, piece in enumerate(pieces):
                if i >= NR:
                    sp.wait_ge(w_split, i - NR + 1)
                sp.dma_start(raw_piece(i), piece[0]).then_inc(w_raw[i % NR], 16)
                if after and i + 1 == min(NR, split_by[after[1]]):
                    load_o(0)
            if cross:
                load_context(0)
            if after:
                sp.wait_ge(r_tile, KT)
                load_o(1)
            with sp.Fori(0, B - 2, 1) as b:
                element(b, order, 2)
            element(B - 2, order, 1)
            element(B - 1, last_order, 0)
            if x_out is not None:
                sp.wait_ge(x_stored, 16 * B)
            if attn:
                for s in range(SPL):
                    if uses[s]:
                        sp.wait_ge(split_stored[s], 1 + 32 * B * uses[s])
                for s in range(VPL):
                    sp.wait_ge(v_stored[s], 1 + 16 * B * v_uses[s])

        @block.gpsimd
        def _(pool):
            pr.clear_old(pool)
            if attn and a.layer == 1:
                pad = v_sb[:].rearrange("p s (h m) -> p (s h) m", m=32)
                nc.gpsimd.memset(pad[:, :, 16:32], 0.0).then_inc(pad_done, 1)
                pool.wait_ge(pad_done, 1)
                nc.gpsimd.memset(pad[:, :, 16:17], 1.0).then_inc(pad_done, 1)

        @block.tensor
        def _(pe):
            def element(b, steps):
                nxt = 0 if b is None else b + 1
                d = ac = 0

                def d_bank():
                    if b is not None:
                        pe.wait_ge(d_read, 1 + d_count(b, max(d - 3, 0)))
                    return ps[:, d % 4, :]

                def a_bank():
                    pe.wait_ge(a_read, 1 + b * NA + max(ac - NAB + 1, 0))
                    return ps[:, 4 + ac % NAB, :]

                def statistic(src):
                    out = d_bank()
                    for kt in range(KT):
                        last = nc.tensor.matmul(out, pr.mean_ones[:], src[:, kt, :],
                                                start=(kt == 0), stop=(kt == KT - 1))
                    last.then_inc(d_tile, 1)

                for kind, m in steps:
                    of = nxt if m == 0 else b
                    if kind == "after":
                        if m == 0:
                            pe.wait_ge(w_split, split_by[after[1]])
                            pe.wait_ge(o_loaded, 32 * (nxt + 1))
                            if b is not None:
                                pe.wait_ge(r_read, KT * nxt)
                        product3(ps[:, 6 + m, :], wo, (slice(m * P, (m + 1) * P),), o, (slice(None),), ko)\
                            .then_inc(r_tile, 1)
                    elif kind == "mean":
                        if m:
                            pe.wait_ge(d_read, 1 + d_count(b, d))
                        elif after:
                            pe.wait_ge(r_read, KT * (nxt + 1))
                        else:
                            pe.wait_ge(x_loaded, 16 * (nxt + 1))
                        statistic(x)
                    elif kind == "var":
                        pe.wait_ge(squared, 2 * ln_no(m, of) + 2)
                        statistic(sq)
                    elif kind == "gate":
                        if m == 0:
                            pe.wait_ge(w_split, split_by[ff[5]])
                            pe.wait_ge(z_done, ln_no(0, b) + 1)
                        g0 = FF * geglu + m * P
                        product3(a_bank(), w1, (slice(g0, g0 + P),), z[0], (slice(None),), KT)\
                            .then_inc(a_tile, 1)
                        if geglu:
                            product3(d_bank(), w1, (slice(m * P, (m + 1) * P),), z[0], (slice(None),), KT)\
                                .then_inc(d_tile, 1)
                    elif kind == "out":
                        pe.wait_ge(u_lo, 1 + (b + 1) * FT)
                        product3(d_bank(), w2, (slice(m * P, (m + 1) * P),), u, (slice(None),), FT)\
                            .then_inc(d_tile, 1)
                    elif kind in ("q", "k", "v"):
                        pe.wait_ge(w_split, len(pieces))
                        if kind == "q" or not cross:
                            pe.wait_ge(z_done, ln_no(last_ln(), b) + 1)
                            src = z[-1]
                        else:
                            pe.wait_ge(ctx_split, b + 1)
                        if kind == "q":
                            product3(d_bank(), wq, (slice(m * P, (m + 1) * P),), src, (slice(None),), KT)\
                                .then_inc(d_tile, 1)
                        elif kind == "k":
                            t, c0, w = k_place(m)
                            rows, cols, out = slice(t * P, (t + 1) * P), slice(c0, c0 + w), d_bank()[:, 0:w]
                            if cross:
                                last = product5(out, wk, rows, c, cols)
                            else:
                                last = product3(out, wk, (rows,), src, (cols,), KT)
                            last.then_inc(d_tile, 1)
                        else:
                            r = a.chunk_rows(m)
                            for hf in range(vhalf):
                                rows, cols = slice(m * P, m * P + r), slice(hf * vw, (hf + 1) * vw)
                                out = a_bank()[0:r, 0:vw]
                                if cross:
                                    last = product5(out, c, rows, wv, cols)
                                else:
                                    last = product3(out, src, (rows,), wv, (cols,), KT)
                                last.then_inc(a_tile, 1)
                                ac += 1
                            ac -= vhalf
                    d += d_tiles(kind)
                    ac += a_tiles(kind)

            element(None, prologue)
            with pe.Fori(0, B - 1, 1) as b:
                element(b, order)
            element(B - 1, last_order)

        @block.scalar
        def _(act):
            def element(b, steps):
                nxt = 0 if b is None else b + 1
                d = ac = 0

                def u_round(m):
                    if geglu:
                        act.wait_ge(d_read, 1 + d_count(b, m + 1))
                    else:
                        act.wait_ge(a_read, 1 + b * NA + m + 1)
                    nc.scalar.copy(u[0][:, m, :], uf[:, m % GR, :]).then_inc(u_hi, 1)

                for kind, m in steps:
                    of = nxt if m == 0 else b
                    if kind == "mean":
                        for n, half in enumerate(HALVES):
                            act.wait_ge(centred, 2 * ln_no(m, of) + n + 1)
                            nc.scalar.activation(sq[:, :, half], xc[:, :, half], ACT.Square).then_inc(squared, 1)
                    elif kind == "scale":
                        for n, half in enumerate(HALVES):
                            act.wait_ge(inverted, 2 * ln_no(m, of) + n + 1)
                            nc.scalar.activation(dev[:, half], var[:, half], ACT.Sqrt).then_inc(rooted, 1)
                    elif kind == "shift":
                        act.wait_ge(d_tile, d_count(b, d))
                        if b is not None and ac:
                            act.wait_ge(a_tile, b * NA + ac)
                        for n, half in enumerate(HALVES):
                            act.wait_ge(scaled, 2 * ln_no(m, of) + n + 1)
                            for kt in range(KT):
                                last = nc.scalar.activation(z[m][0][:, kt, half], ud[:, kt, half], ACT.Identity,
                                                            bias=pr.vcol(ln_vectors[m][1], kt))
                            last.then_inc(z_hi_done, 1)
                    elif kind == "gate":
                        act.wait_ge(a_tile, b * NA + ac + 1)
                        if geglu:
                            act.wait_ge(d_read, 1 + d_count(b, max(m - 1, 0)))
                        else:
                            act.wait_ge(u_lo, 1 + b * FT + max(m - GR + 1, 0))
                        nc.scalar.activation(gate[:, m % GR, :], ps[:, 4 + ac % NAB, :], ACT.Gelu,
                                             bias=pr.vcol(ff[4], FT * geglu + m)).then_inc(a_read, 1)
                        if m:
                            u_round(m - 1)
                    elif kind == "gate_end":
                        u_round(FT - 1)
                    elif kind == "context":
                        act.wait_ge(ctx_loaded, 16 * (b + 1))
                        nc.scalar.copy(c[0][:], ctx_raw[:]).then_inc(ctx_hi_done, 1)
                    elif kind in ("q", "k"):
                        n, w = split_no[kind, m], NQ if kind == "q" else k_place(m)[2]
                        act.wait_ge(d_tile, d_count(b, d) + 1)
                        act.wait_ge(split_stored[n % SPL], 1 + 32 * (b * uses[n % SPL] + n // SPL))
                        nc.scalar.copy(sp_hi[:, n % SPL, 0:w], ps[:, d % 4, 0:w]).then_inc(hi_done, 1)
                    elif kind == "v":
                        if a.layer == 1:
                            act.wait_ge(pad_done, 2)
                        r = a.chunk_rows(m)
                        act.wait_ge(v_stored[m % VPL], 1 + 16 * (b * v_uses[m % VPL] + m // VPL))
                        for hf in range(vhalf):
                            act.wait_ge(a_tile, b * NA + ac + hf + 1)
                            src = ps[0:r, 4 + (ac + hf) % NAB, 0:vw]
                            if a.layer == 0:
                                dst = v_sb[0:r, m % VPL, hf * vw:(hf + 1) * vw]
                            else:
                                dst = v_sb[0:r, m % VPL, :].rearrange("p (h m) -> p h m", m=32)[:, :, 0:16]
                                src = src.rearrange("p (h m) -> p h m", m=16)
                            nc.scalar.copy(dst, src).then_inc(a_read, 1)
                    d += d_tiles(kind)
                    ac += a_tiles(kind)

            act.sem_inc(a_read, 1)
            for i in range(len(pieces)):
                act.wait_ge(w_raw[i % NR], 16 * (i // NR + 1))
                nc.scalar.copy(pieces[i][1], raw_piece(i)).then_inc(w_hi, 1)
            act.wait_ge(w_split, len(pieces))
            element(None, prologue)
            with act.Fori(0, B - 1, 1) as b:
                element(b, order)
            element(B - 1, last_order)

        @block.vector
        def _(dve):
            def element(b, steps):
                nxt = 0 if b is None else b + 1
                d = 0

                def tile_here():
                    dve.wait_ge(d_tile, d_count(b, d) + 1)
                    return ps[:, d % 4, :]

                def u_low(m):
                    dve.wait_ge(u_hi, b * FT + m + 1)
                    nc.vector.tensor_tensor(u[1][:, m, :], uf[:, m % GR, :], u[0][:, m, :].bitcast(F32),
                                            ALU.subtract).then_inc(u_lo, 1)

                for kind, m in steps:
                    of = nxt if m == 0 else b
                    if kind == "residual":
                        dve.wait_ge(x_loaded, 16 * (nxt + 1))
                        if b is not None:
                            dve.wait_ge(x_stored, 16 * nxt)
                        for t in range(KT):
                            dve.wait_ge(r_tile, KT * nxt + t + 1)
                            nc.vector.scalar_tensor_tensor(out=x[:, t, :], in0=ps[:, 6 + t, :],
                                                           scalar=pr.vcol(after[2], t), in1=x_from[:, t, :],
                                                           op0=ALU.add, op1=ALU.add).then_inc(r_read, 1)
                    elif kind == "mean":
                        mean = tile_here()
                        for half in HALVES:
                            for kt in range(KT):
                                last = nc.vector.tensor_tensor(xc[:, kt, half], x[:, kt, half], mean[:, half],
                                                               ALU.subtract)
                            last.then_inc(centred, 1)
                        dve.wait_ge(centred, 2 * ln_no(m, of) + 2)
                        dve.sem_inc(d_read, 1)
                    elif kind == "var":
                        nc.vector.tensor_scalar(var[:], tile_here(), EPS, None, ALU.add).then_inc(d_read, 1)
                        dve.wait_ge(d_read, 1 + d_count(b, d) + 1)
                        for half in HALVES:
                            nc.vector.reciprocal(var[:, half], var[:, half]).then_inc(inverted, 1)
                    elif kind == "scale":
                        for n, half in enumerate(HALVES):
                            dve.wait_ge(rooted, 2 * ln_no(m, of) + n + 1)
                            for kt in range(KT):
                                last = nc.vector.scalar_tensor_tensor(
                                    out=ud[:, kt, half], in0=xc[:, kt, half],
                                    scalar=pr.vcol(ln_vectors[m][0], kt), in1=dev[:, half],
                                    op0=ALU.mult, op1=ALU.mult)
                            last.then_inc(scaled, 1)
                    elif kind == "shift":
                        for n, half in enumerate(HALVES):
                            dve.wait_ge(z_hi_done, 2 * ln_no(m, of) + n + 1)
                            for kt in range(KT):
                                last = nc.vector.scalar_tensor_tensor(
                                    out=z[m][1][:, kt, half], in0=ud[:, kt, half],
                                    scalar=pr.vcol(ln_vectors[m][1], kt), in1=z[m][0][:, kt, half].bitcast(F32),
                                    op0=ALU.add, op1=ALU.subtract)
                        last.then_inc(z_done, 1)
                    elif kind == "gate":
                        if geglu:
                            t = tile_here()
                            dve.wait_ge(a_read, 1 + b * NA + m + 1)
                            dve.wait_ge(u_lo, 1 + b * FT + max(m - 1, 0))
                            nc.vector.scalar_tensor_tensor(
                                out=uf[:, m % GR, :], in0=t, scalar=pr.vcol(ff[4], m), in1=gate[:, m % GR, :],
                                op0=ALU.add, op1=ALU.mult).then_inc(d_read, 1)
                        if m:
                            u_low(m - 1)
                    elif kind == "gate_end":
                        u_low(FT - 1)
                    elif kind == "context":
                        dve.wait_ge(ctx_hi_done, b + 1)
                        nc.vector.tensor_tensor(c[1][:], ctx_raw[:], c[0][:].bitcast(F32),
                                                ALU.subtract).then_inc(ctx_split, 1)
                    elif kind == "out":
                        nc.vector.scalar_tensor_tensor(out=x[:, m, :], in0=tile_here(), scalar=pr.vcol(ff[6], m),
                                                       in1=x[:, m, :], op0=ALU.add, op1=ALU.add)\
                            .then_inc(d_read, 1)
                    elif kind in ("q", "k"):
                        n, w = split_no[kind, m], NQ if kind == "q" else k_place(m)[2]
                        t = tile_here()
                        dve.wait_ge(hi_done, b * NSPLIT + n + 1)
                        nc.vector.tensor_tensor(sp_lo[:, n % SPL, 0:w], t[:, 0:w],
                                                sp_hi[:, n % SPL, 0:w].bitcast(F32), ALU.subtract)\
                            .then_inc(d_read, 1)
                    d += d_tiles(kind)

            dve.sem_inc(d_read, 1)
            dve.sem_inc(u_lo, 1)
            for i in range(len(pieces)):
                dve.wait_ge(w_hi, i + 1)
                hi, lo, stacked = pieces[i][1], pieces[i][2], pieces[i][6]
                if stacked:
                    nc.vector.tensor_tensor(hi[CREST:P], raw_piece(i)[CREST:P], hi[CREST:P].bitcast(F32),
                                            ALU.subtract).then_inc(w_split, 1)
                else:
                    nc.vector.tensor_tensor(lo, raw_piece(i), hi.bitcast(F32), ALU.subtract).then_inc(w_split, 1)
            dve.wait_ge(w_split, len(pieces))
            element(None, prologue)
            with dve.Fori(0, B - 1, 1) as b:
                element(b, order)
            element(B - 1, last_order)


def attend_phase(pr, name, a):
    nc = pr.nc
    pr.start_phase()
    G, M, NC, NCP, U, NG, KP, NB, S = a.G, a.M, a.NC, a.NCP, a.U, a.NG, a.kp, a.NB, a.keys
    wide = a.layer == 0
    SLOTS = 3 if a.cross else 4
    RC = SLOTS
    IH = 4 * NB
    NI = IH * G
    NLOAD = 4 if wide else 8
    NLOAD2 = (3 if wide else 1) + (NC * P > S)
    PIECE = P
    E = NC * G
    MXB, SCB = (3, 3) if a.cross else (4, 2)
    assert SLOTS * NI % MXB == 0 and SLOTS * E % SCB == 0

    def chunk_step(cp, h, k):
        return 2 * G * cp + len(a.pair(cp)) * h + k

    def items_until(u):
        return min(NI, -(-(u + 1) * NI // (U - 1)))

    row_at = [min(U - 1, next(u for u in range(U) if items_until(u) >= (h + 1) * IH) + 1) for h in range(G)]
    row_at[G - 1] = U

    def value_at(j):
        return j // 2 * G + G + 1 + j % 2 * (G // 2)

    RAW_AT = value_at(NC - 1) + 1
    MERGE_AT = U + 1
    DEN_AT = U + 3 if wide else RAW_AT + 2
    DEN_COPY_AT = SPREAD_AT = INVERT_AT = DEN_AT + 1
    if wide and NCP > 2:
        RECIP_AT = [DEN_AT + 2 + k for k in range(4)]
        DIVIDE_AT = RECIP_AT[3] + 1
    elif wide:
        RECIP_AT, DIVIDE_AT = [DEN_AT + 2, DEN_AT + 4, DEN_AT + 4, DEN_AT + 5], DEN_AT + 5
    else:
        DIVIDE_AT = DEN_AT + 2
    HIGH_AT = DIVIDE_AT + 1
    LOW_AT = HIGH_AT + 1
    PEEL = max(2, LOW_AT // U)
    assert LOW_AT < (PEEL + 1) * U
    DEN_BACK, DEN_U = DEN_AT // U, DEN_AT % U
    assert wide or DEN_U + 1 not in row_at
    early_rows = sum(p <= DEN_U for p in row_at)

    pool_sums = [(cp, h) for cp in range(1, min(NCP, 6)) for h in range(G)]
    dve_sums = [(cp, h) for cp in range(6, NCP) for h in range(G)] if wide else []

    def sem(what):
        return pr.sem(f"{name}_{what}")

    loaded = [sem(f"loaded{r}") for r in range(SLOTS)]
    loaded2 = [sem(f"loaded_second{r}") for r in range(SLOTS)]
    zeros_set, first_zeros, ones_set = sem("zeros_set"), sem("first_zeros"), sem("ones_set")
    item_done, item_read, max_done = sem("item_done"), sem("item_read"), sem("max_done")
    row_done, row_copied = sem("row_done"), sem("row_copied")
    st_done, exp_done, pv_done, pv_copied = sem("st_done"), sem("exp_done"), sem("pv_done"), sem("pv_copied")
    pool_sum, dve_sum, merged = sem("pool_sum"), sem("dve_sum"), sem("merged")
    den_done, den_copied, inverted, divided = sem("den_done"), sem("den_copied"), sem("inverted"), sem("divided")
    spread = sem("spread")
    aux_read = den_copied if wide else divided
    o_hi_done, o_lo_done = sem("o_hi_done"), sem("o_lo_done")
    o_stored = [sem(f"o_stored{s}") for s in range(SLOTS)]

    with ExitStack() as st:
        def sb(what, shape, dt=F32):
            return st.enter_context(nc.sbuf_tensor(f"{name}_{what}", shape, dt))

        MR = 64 if wide else 96
        ROWS = 65 if wide else P
        kst = [sb(f"k_stack{r}", [P, G, KP], F32R) for r in range(SLOTS)]
        qst = [sb(f"q_stack{r}", [P, G, NQ], F32R) for r in range(SLOTS)]
        k2 = [sb(f"k_second{r}", [65, G, KP], F32R) for r in range(SLOTS)] if wide else kst
        q2 = [sb(f"q_second{r}", [65, G, NQ], F32R) for r in range(SLOTS)] if wide else qst
        v = [sb(f"v{r}", [P, NC, P]) for r in range(SLOTS)]
        prob = sb("prob", [P, RC, G, 2, BANK])
        blk_max = sb("blk_max", [P, SLOTS, G, 4, NB])
        row_max = sb("row_max", [P, SLOTS, G, 4, 1]) if NB > 1 else blk_max
        if wide:
            prob_sum = sb("prob_sum", [P, G, 2, BANK])
            chunk_sum = sb("chunk_sum", [P, G, NQ])
        if wide:
            den = sb("den", [P, SLOTS, NQ])
        else:
            inv_cols = sb("inv_cols", [P, SLOTS, 4 * G])
        o_full = sb("o_full", [P, SLOTS, NQ])
        o_hi, o_lo = sb("o_hi", [P, SLOTS, NQ], F32R), sb("o_lo", [P, SLOTS, NQ], F32R)
        mx = st.enter_context(nc.psum_tensor(f"{name}_mx", [P, MXB, BANK], F32))
        sc = st.enter_context(nc.psum_tensor(f"{name}_sc", [P, SCB, BANK], F32))
        pv = st.enter_context(nc.psum_tensor(f"{name}_pv", [P, BANK], F32))
        aux = st.enter_context(nc.psum_tensor(f"{name}_aux", [P, BANK], F32))
        block = st.enter_context(nc.Block())

        def prob_of(c, cp, h):
            return prob[:, (c * NCP + cp) % RC, h]

        def groups(eng, body, end):
            for i in range(PEEL):
                body(i // SLOTS, i % SLOTS, i)
            rounds = (NG - PEEL - end) // SLOTS
            with eng.Fori(0, rounds, 1) as q:
                for c in range(PEEL, PEEL + SLOTS):
                    body(q, c, None)
            for i in range(PEEL + SLOTS * rounds, NG):
                body(i // SLOTS, i % SLOTS, i)

        def late(u, at):
            return at // U if at % U == u else 0

        def exists(n, back):
            return n is None or n >= back

        def drain(steps):
            todo = [(g * U + at, g, step) for at, step in steps for g in range(NG - PEEL, NG)
                    if g * U + at >= NG * U]
            for _, g, step in sorted(todo, key=lambda x: x[0]):
                step(g // SLOTS, g % SLOTS)

        @block.sync
        def _(sp):
            def load(q, c):
                r, one = c % SLOTS, bass.ds(SLOTS * q + c, 1)
                k_hi, k_lo = (t[one].rearrange("g (h r) s -> r (g h) s", h=G) for t in pr.k[a.name])
                q_hi, q_lo = (t[one].rearrange("g (h r) s -> r (g h) s", h=G) for t in pr.q[a.name])
                if wide:
                    moves = [(kst[r][0:64], k_hi), (kst[r][64:128], k_lo), (qst[r][0:64], q_hi),
                             (qst[r][64:128], q_hi), (k2[r][0:64], k_hi), (q2[r][0:64], q_lo)]
                else:
                    moves = [(kst[r][16 * n:16 * n + 16], (k_hi, k_lo)[n % 2]) for n in range(4)]
                    moves += [(qst[r][16 * n:16 * n + 16], (q_hi, q_lo)[n // 2]) for n in range(4)]
                vs = pr.v[a.name][one].rearrange("g p c m -> (g p) c m")
                full = S // P
                moves.append((v[r][:, 0:full, :], vs[:, 0:full, :]))
                if full < NC:
                    rows = a.chunk_rows(full)
                    moves.append((v[r][0:rows, full:NC, :], vs[0:rows, full:NC, :]))
                assert len(moves) == NLOAD + NLOAD2
                for m, (dst, src) in enumerate(moves):
                    sp.dma_start(words(dst), src).then_inc(loaded[r] if m < NLOAD else loaded2[r], 16)

            def store(q, c):
                r, i = c % SLOTS, SLOTS * q + c
                sp.wait_ge(o_lo_done, i + 1)
                for dst, src in zip(pr.o[a.name], (o_hi, o_lo)):
                    sp.dma_start(dst[bass.ds(i, 1)].rearrange("i p n -> (i p) n"), words(src[:, r, :]))\
                        .then_inc(o_stored[r], 16)

            def main(q, c, n):
                if n != 0:
                    sp.wait_ge(pv_done, (SLOTS * q + c) * NC)
                if n is None or n + SLOTS - 1 < NG:
                    load(q, c + SLOTS - 1)
                if exists(n, LOW_AT // U):
                    store(q, c - LOW_AT // U)

            for stored in o_stored:
                sp.sem_inc(stored, 1)
            for g in range(SLOTS - 1):
                load(0, g)
            groups(sp, main, SLOTS - 1)
            for g in range(NG - LOW_AT // U, NG):
                store(g // SLOTS, g % SLOTS)
            for r in range(SLOTS):
                sp.wait_ge(o_stored[r], 1 + 32 * len(range(r, NG, SLOTS)))

        @block.gpsimd
        def _(pool):
            pr.clear_old(pool)
            for r in range(SLOTS):
                if not wide and r == 0:
                    pool.wait_ge(first_zeros, 2)
                elif not wide:
                    nc.gpsimd.memset(kst[r][64:P].bitcast(F32), 0.0).then_inc(zeros_set, 1)
                    nc.gpsimd.memset(qst[r][64:P].bitcast(F32), 0.0).then_inc(zeros_set, 1)
                    pool.wait_ge(zeros_set, 2 * r)
                nc.gpsimd.memset(k2[r][MR:MR + 1].bitcast(F32), 1.0).then_inc(ones_set, 1)
                pool.wait_ge(ones_set, r + 1)

            def main(q, c, n):
                i = SLOTS * q + c
                for m, (cp, h) in enumerate(pool_sums):
                    pool.wait_ge(exp_done, i * E + chunk_step(cp, h + 1, 0))
                    if cp == 1:
                        if n != 0:
                            pool.wait_ge(merged, (i - 1) * G + h + 1)
                        other = prob_of(c, 0, h)
                    else:
                        pool.wait_ge(pool_sum, i * len(pool_sums) + m - G + 1)
                        other = prob_sum[:, h]
                    nc.gpsimd.tensor_tensor(prob_sum[:, h], prob_of(c, cp, h), other, ALU.add)\
                        .then_inc(pool_sum, 1)
                    if NCP == 2:
                        pool.wait_ge(pool_sum, i * len(pool_sums) + m + 1)
                        if n != 0:
                            pool.wait_ge(den_done, i)
                        nc.gpsimd.tensor_tensor(chunk_sum[:, h, :], prob_sum[:, h, 0, :], prob_sum[:, h, 1, :],
                                                ALU.add).then_inc(merged, 1)

            if wide:
                groups(pool, main, 1)

        @block.tensor
        def _(pe):
            def item(q, c, n, m):
                r, i = c % SLOTS, SLOTS * q + c
                if m == 0:
                    pe.wait_ge(loaded[r], 16 * NLOAD * (q + c // SLOTS + 1))
                rows = P if wide else 96
                h, t, at = m // IH, m % IH // NB, a.block_at[m % NB]
                if not (n == 0 and m < MXB):
                    pe.wait_ge(item_read, i * NI + m - MXB + 1)
                nc.tensor.matmul(mx[:, (c * NI + m) % MXB, 0:a.blk], qst[r][0:rows, h, t * P:(t + 1) * P],
                                 kst[r][0:rows, h, at:at + a.blk], start=True, stop=True)\
                    .then_inc(item_done, 1)

            def row(q, c, h, n, dens):
                r, i = c % SLOTS, SLOTS * q + c
                if NB > 1:
                    pe.wait_ge(max_done, i * G + h + 1)
                else:
                    pe.wait_ge(item_read, i * NI + (h + 1) * IH)
                if not (n == 0 and h == 0):
                    pe.wait_ge(row_copied, i * G + h)
                if not (isinstance(dens, int) and dens <= 0):
                    pe.wait_ge(aux_read, dens)
                for t in range(4):
                    last = nc.tensor.transpose(aux[0:1, t * P:(t + 1) * P], row_max[:, r, h, t], pr.ident[:])
                last.then_inc(row_done, 1)

            def scores(q, c, u, k, n):
                r, cp, h = c % SLOTS, u // G, u % G
                ch, e = 2 * cp + k, chunk_step(cp, h, k)
                rows, k0 = a.chunk_rows(ch), ch * P
                if not (n == 0 and e < SCB):
                    pe.wait_ge(exp_done, (SLOTS * q + c) * E + e - SCB + 1)
                out = sc[0:rows, (c * E + e) % SCB, :]
                if wide:
                    nc.tensor.matmul(out, kst[r][:, h, k0:k0 + rows], qst[r][:, h, :], start=True, stop=False)
                nc.tensor.matmul(out, k2[r][0:ROWS, h, k0:k0 + rows], q2[r][0:ROWS, h, :],
                                 start=not wide, stop=True).then_inc(st_done, 1)

            def values(q, c, j):
                r, i, cp = c % SLOTS, SLOTS * q + c, j // 2
                pe.wait_ge(exp_done, i * E + min(NC, 2 * cp + 2) * G)
                if j == 0 and not (isinstance(i, int) and i == 0):
                    pe.wait_ge(pv_copied, i)
                rows = a.chunk_rows(j)
                for h in range(G):
                    last = nc.tensor.matmul(pv[h * M:(h + 1) * M, :], v[r][0:rows, j, h * M:(h + 1) * M],
                                            prob_of(c, cp, h)[0:rows, j % 2, :],
                                            start=(j == 0), stop=(j == NC - 1))
                last.then_inc(pv_done, 1)

            def denominators(q, c, rows_before):
                r, i = c % SLOTS, SLOTS * q + c
                pe.wait_ge(row_copied, rows_before)
                if DEN_BACK > 1 or not isinstance(i, int) or i:
                    if not (isinstance(i, int) and i == 0):
                        pe.wait_ge(aux_read, i)
                if wide:
                    pe.wait_ge(merged, (i + 1) * G)
                    for h in range(G):
                        last = nc.tensor.matmul(aux[h * M:(h + 1) * M, :], pr.ones[:, 0:M],
                                                chunk_sum[:, h, :], start=True, stop=True)
                else:
                    pe.wait_ge(pv_copied, i + 1)
                    for t in range(4):
                        last = nc.tensor.matmul(aux[:, t * G:(t + 1) * G], o_full[:, r, t * P:(t + 1) * P],
                                                pr.den_pick[:], start=True, stop=True)
                last.then_inc(den_done, 1)

            def spread_inverses(q, c):
                r = c % SLOTS
                pe.wait_ge(inverted, SLOTS * q + c + 1)
                for t in range(4):
                    for h in range(G):
                        of_rows = inv_cols[:, r, t * G + h:t * G + h + 1].to_broadcast([P, M])
                        last = nc.tensor.matmul(aux[h * M:(h + 1) * M, t * P:(t + 1) * P], of_rows, pr.ident[:],
                                                start=True, stop=True)
                last.then_inc(spread, 1)

            def main(q, c, n):
                i, ahead, done = SLOTS * q + c, n != NG - 1, 0
                pe.wait_ge(loaded2[c % SLOTS], 16 * NLOAD2 * (q + c // SLOTS + 1))
                if n == 0:
                    pe.wait_ge(ones_set, 2)
                elif n == 1:
                    pe.wait_ge(ones_set, SLOTS)
                for u in range(U):
                    todo = list(range(done, items_until(u))) if ahead else []
                    done = items_until(u)

                    def next_item():
                        if todo:
                            item(q, c + 1, None, todo.pop(0))

                    if u < G:
                        pe.wait_ge(row_copied, i * G + u + 1)
                    for k in range(len(a.pair(u // G))):
                        scores(q, c, u, k, n)
                        next_item()
                    if u == 0:
                        row(q, c, G - 1, n, i - DEN_BACK)
                    if ahead:
                        for h in range(G):
                            if row_at[h] == u:
                                row(q, c + 1, h, None, i - DEN_BACK + (DEN_U < u))
                    for j in range(NC):
                        back = value_at(j) // U
                        if value_at(j) % U == u and exists(n, back):
                            values(q, c - back, j)
                            next_item()
                    while todo:
                        next_item()
                    if DEN_U == u and exists(n, DEN_BACK):
                        denominators(q, c - DEN_BACK, (i + 1) * G + (early_rows if ahead else 0))
                    if not wide and late(u, SPREAD_AT) and exists(n, late(u, SPREAD_AT)):
                        spread_inverses(q, c - late(u, SPREAD_AT))

            if not wide:
                pe.wait_ge(first_zeros, 2)
            for m in range(NI):
                item(0, 0, 0, m)
            for h in range(G - 1):
                row(0, 0, h, 0, 0)
            groups(pe, main, 1)
            drain([(value_at(j), lambda q, c, j=j: values(q, c, j)) for j in range(NC)]
                  + [(DEN_AT, lambda q, c: denominators(q, c, NG * G))]
                  + [(SPREAD_AT, spread_inverses)] * (not wide))

        @block.scalar
        def _(act):
            def row_copy(q, c, h):
                r, i = c % SLOTS, SLOTS * q + c
                act.wait_ge(row_done, i * G + h + 1)
                nc.scalar.activation(q2[r][MR:MR + 1, h, :], aux[0:1, :], ACT.Copy, scale=-1.0)\
                    .then_inc(row_copied, 1)

            def exps(q, c, u, known):
                i, cp, h = SLOTS * q + c, u // G, u % G
                back, cpb = -((cp - RC) // NCP), (cp - RC) % NCP
                if exists(known, back):
                    act.wait_ge(pv_done, (i - back) * NC + min(NC, 2 * cpb + 2))
                    if wide:
                        unit = (max(cpb, 1), h)
                        if unit in pool_sums:
                            act.wait_ge(pool_sum, (i - back) * len(pool_sums) + pool_sums.index(unit) + 1)
                        else:
                            act.wait_ge(dve_sum, (i - back) * len(dve_sums) + dve_sums.index(unit) + 1)
                for k, ch in enumerate(a.pair(cp)):
                    rows, e = a.chunk_rows(ch), chunk_step(cp, h, k)
                    act.wait_ge(st_done, i * E + e + 1)
                    nc.scalar.activation(prob_of(c, cp, h)[0:rows, k, :], sc[0:rows, (c * E + e) % SCB, :],
                                         ACT.Exp, scale=a.scale).then_inc(exp_done, 1)

            def raw_copy(q, c):
                i = SLOTS * q + c
                act.wait_ge(pv_done, (i + 1) * NC)
                nc.scalar.copy(o_full[:, c % SLOTS, :], pv[:]).then_inc(pv_copied, 1)

            def den_copy(q, c):
                i = SLOTS * q + c
                act.wait_ge(den_done, i + 1)
                nc.scalar.copy(den[:, c % SLOTS, :], aux[:]).then_inc(den_copied, 1)

            def high_part(q, c):
                i = SLOTS * q + c
                act.wait_ge(divided, i + 1)
                if not (isinstance(i, int) and i < SLOTS):
                    act.wait_ge(o_stored[c % SLOTS], 1 + 32 * (q + c // SLOTS))
                nc.scalar.copy(o_hi[:, c % SLOTS, :], o_full[:, c % SLOTS, :]).then_inc(o_hi_done, 1)

            steps = [(RAW_AT, raw_copy)] + [(DEN_COPY_AT, den_copy)] * wide + [(HIGH_AT, high_part)]

            def main(q, c, n):
                for u in range(U):
                    for at, step in steps:
                        if late(u, at) and exists(n, late(u, at)):
                            step(q, c - late(u, at))
                    exps(q, c, u, n)
                    if u == 0:
                        row_copy(q, c, G - 1)
                    if n != NG - 1:
                        for h in range(G):
                            if row_at[h] == u:
                                row_copy(q, c + 1, h)

            for h in range(G - 1):
                row_copy(0, 0, h)
            groups(act, main, 1)
            drain(steps)

        @block.vector
        def _(dve):
            def items(q, c, done, until):
                r, i = c % SLOTS, SLOTS * q + c
                for n in range(done, until):
                    h, t, nb = n // IH, n % IH // NB, n % NB
                    dve.wait_ge(item_done, i * NI + n + 1)
                    nc.vector.reduce_max(blk_max[:, r, h, t, nb:nb + 1], mx[:, (c * NI + n) % MXB, 0:a.blk], AX.X)\
                        .then_inc(item_read, 1)
                    if NB > 1 and n % IH == IH - 1:
                        dve.wait_ge(item_read, i * NI + n + 1)
                        nc.vector.reduce_max(row_max[:, r, h, :, 0], blk_max[:, r, h], AX.X)\
                            .then_inc(max_done, 1)

            def last_sums(q, c):
                i = SLOTS * q + c
                for n, (cp, h) in enumerate(dve_sums):
                    rows = a.chunk_rows(2 * cp)
                    dve.wait_ge(exp_done, i * E + chunk_step(cp, h + 1, 0))
                    dve.wait_ge(pool_sum, i * len(pool_sums) + len(pool_sums) - G + h + 1)
                    nc.vector.tensor_tensor(prob_sum[0:rows, h, 0, :], prob_sum[0:rows, h, 0, :],
                                            prob_of(c, cp, h)[0:rows, 0, :], ALU.add).then_inc(dve_sum, 1)

            def merge(q, c):
                i = SLOTS * q + c
                if not (isinstance(i, int) and i == 0):
                    dve.wait_ge(den_done, i)
                for h in range(G):
                    dve.wait_ge(pool_sum, i * len(pool_sums) + len(pool_sums) - G + h + 1)
                    dve.wait_ge(dve_sum, i * len(dve_sums) + h + 1)
                    nc.vector.tensor_tensor(chunk_sum[:, h, :], prob_sum[:, h, 0, :], prob_sum[:, h, 1, :],
                                            ALU.add).then_inc(merged, 1)

            def invert(q, c, k):
                dve.wait_ge(den_copied, SLOTS * q + c + 1)
                piece = den[:, c % SLOTS, k * PIECE:(k + 1) * PIECE]
                nc.vector.reciprocal(piece, piece).then_inc(inverted, 1)

            def invert_columns(q, c):
                dve.wait_ge(den_done, SLOTS * q + c + 1)
                nc.vector.reciprocal(inv_cols[:, c % SLOTS, :], aux[:, 0:4 * G]).then_inc(inverted, 1)

            def divide(q, c):
                i = SLOTS * q + c
                if wide:
                    dve.wait_ge(inverted, 4 * (i + 1))
                    inv = den[:, c % SLOTS, :]
                else:
                    dve.wait_ge(spread, i + 1)
                    inv = aux[:]
                dve.wait_ge(pv_copied, i + 1)
                nc.vector.tensor_tensor(o_full[:, c % SLOTS, :], o_full[:, c % SLOTS, :], inv, ALU.mult)\
                    .then_inc(divided, 1)

            def low_part(q, c):
                i = SLOTS * q + c
                dve.wait_ge(o_hi_done, i + 1)
                if not (isinstance(i, int) and i < SLOTS):
                    dve.wait_ge(o_stored[c % SLOTS], 1 + 32 * (q + c // SLOTS))
                nc.vector.tensor_tensor(o_lo[:, c % SLOTS, :], o_full[:, c % SLOTS, :],
                                        o_hi[:, c % SLOTS, :].bitcast(F32), ALU.subtract).then_inc(o_lo_done, 1)

            steps = [(U, last_sums), (MERGE_AT, merge)] * bool(dve_sums)
            if wide:
                steps += [(at, lambda q, c, k=k: invert(q, c, k)) for k, at in enumerate(RECIP_AT)]
            else:
                steps += [(INVERT_AT, invert_columns)]
            steps += [(DIVIDE_AT, divide), (LOW_AT, low_part)]

            def main(q, c, n):
                done = 0
                for u in range(U):
                    extra = [(step, late(u, at)) for at, step in steps if late(u, at) and exists(n, late(u, at))]
                    until = items_until(u)
                    if not wide and extra and extra[0][0] is not low_part:
                        step, back = extra.pop(0)
                        step(q, c - back)
                    while extra or (done < until and n != NG - 1):
                        if done < until and n != NG - 1:
                            items(q, c + 1, done, done + 1)
                            done += 1
                        if extra:
                            step, back = extra.pop(0)
                            step(q, c - back)

            if not wide:
                for t in (kst[0], qst[0]):
                    nc.vector.memset(t[64:P].bitcast(F32), 0.0).then_inc(first_zeros, 1)
            items(0, 0, 0, NI)
            groups(dve, main, 1)
            drain(steps)


def build(nc, ins, out):
    with ExitStack() as keep:
        pr = Program(nc, ins, out, keep)
        w0, w1 = "L0_xattn_", "L1_xattn_"
        setup_phase(pr)
        project_phase(pr, "p0", x_in=ins["x"],
                      attn=(SELF0, w0 + "g1", w0 + "b1", w0 + "Wq1", w0 + "Wk1", w0 + "Wv1"))
        attend_phase(pr, "a0", SELF0)
        project_phase(pr, "p1", x_in=ins["x"], x_out=pr.x, after=(SELF0, w0 + "Wo1", w0 + "bo1"),
                      attn=(CROSS0, w0 + "g2", w0 + "b2", w0 + "Wq2", w0 + "Wk2", w0 + "Wv2"))
        attend_phase(pr, "a1", CROSS0)
        project_phase(pr, "p2", x_in=pr.x, x_out=pr.x, after=(CROSS0, w0 + "Wo2", w0 + "bo2"),
                      ff=("geglu", w0 + "g3", w0 + "b3", w0 + "Wp", w0 + "bp", w0 + "Wf", w0 + "bf"),
                      attn=(SELF1, w1 + "n1_g", w1 + "n1_b", w1 + "sq_w", w1 + "sk_w", w1 + "sv_w"))
        attend_phase(pr, "a2", SELF1)
        project_phase(pr, "p3", x_in=pr.x, x_out=pr.x, after=(SELF1, w1 + "so_w", w1 + "so_b"),
                      ff=("gelu", w1 + "n2_g", w1 + "n2_b", w1 + "f1_w1", w1 + "f1_b1", w1 + "f1_w2", w1 + "f1_b2"),
                      attn=(CROSS1, w1 + "n3_g", w1 + "n3_b", w1 + "cq_w", w1 + "ck_w", w1 + "cv_w"))
        attend_phase(pr, "a3", CROSS1)
        project_phase(pr, "p4", x_in=pr.x, x_out=out, after=(CROSS1, w1 + "co_w", w1 + "co_b"),
                      ff=("gelu", w1 + "n4_g", w1 + "n4_b", w1 + "f2_w1", w1 + "f2_b1", w1 + "f2_w2", w1 + "f2_b2"))


_WEIGHTS = (["L0_xattn_" + w for w in ("Wq1", "Wk1", "Wv1", "Wo1", "Wq2", "Wk2", "Wv2", "Wo2", "Wp", "Wf")]
            + ["L1_xattn_" + w for w in ("sq_w", "sk_w", "sv_w", "so_w", "cq_w", "ck_w", "cv_w", "co_w",
                                         "f1_w1", "f1_w2", "f2_w1", "f2_w2")])


def kernel(**inputs):
    import numpy as _np
    import concourse.bacc as _bacc
    from concourse import mybir as _mybir
    from concourse.bass_utils import run_bass_kernel_spmd as _run

    arr = {k: _np.asarray(v) for k, v in inputs.items()}

    def feature_major(t, p):
        return _np.ascontiguousarray(t.reshape(B, t.shape[1], -1, p).transpose(0, 3, 2, 1))

    arrays = {"x": feature_major(arr["x"], P)}
    twice = _np.r_[0:CTX, P:CTX]
    ctx = _np.zeros((B, SCP, CROWS), arr["ctx_768"].dtype)
    ctx[:, :SC] = arr["ctx_768"][:, :, twice]
    arrays["ctx"] = feature_major(ctx, P)
    arrays["vec"] = _np.ascontiguousarray(
        _np.concatenate([arr[n].reshape(w, P) for n, w in VECTORS]).T)
    for n in _WEIGHTS:
        w = arr[n]
        if n in ("L1_xattn_so_w", "L1_xattn_co_w"):
            wide = _np.zeros((HEADS, 32, DIM), w.dtype)
            wide[:, :16] = w.reshape(HEADS, 16, DIM)
            w = wide.reshape(HEADS * 32, DIM)
        if w.shape[0] == CTX:
            w = w[twice]
        arrays[n] = _np.ascontiguousarray(w)

    nc = _bacc.Bacc("TRN2", target_bir_lowering=False, num_devices=1)
    ins = {n: nc.dram_tensor(n + "_in", t.shape, _mybir.dt.from_np(t.dtype), kind="ExternalInput").ap()
           for n, t in arrays.items()}
    out = nc.dram_tensor("out_x", (B, P, KT, NQ), F32, kind="ExternalOutput").ap()
    build(nc, ins, out)
    r = _run(nc, [{n + "_in": t for n, t in arrays.items()}], core_ids=[0])
    got = r.results[0]["out_x"]
    return _np.ascontiguousarray(got.transpose(0, 3, 2, 1).reshape(B, NQ, DIM))
```
